# Optimizing a Trainium2 kernel written in Bass

```python
import numpy as np
import jax
import jax.numpy as jnp

def _softmax(x, axis=-1):
    return jax.nn.softmax(x, axis=axis)
def _gelu(x):
    return jax.nn.gelu(x, approximate=True)
def _silu(x):
    return jax.nn.silu(x)
def _sigmoid(x):
    return jax.nn.sigmoid(x)
def _layernorm(x, axis=-1, eps=1e-5):
    m = jnp.mean(x, axis=axis, keepdims=True)
    v = jnp.var(x, axis=axis, keepdims=True)
    return (x - m) / jnp.sqrt(v + eps)
def _scatter_add(tgt, idx, src, axis=0):
    return tgt.at[idx].add(src)
def _segment_sum(src, seg, n):
    return jax.ops.segment_sum(src, seg, n)

kernel_name = 'mk_conv_preact_d2_conv_nchw512_f8c2ad'

def setup_inputs(seed: int = 0):
    np.random.seed(seed)
    _w = jnp.asarray
    def _rec_inputs():
        import jax
        import jax.numpy as jnp
        _gk = jax.random.key(seed)
        x = -0.000125 + 0.9999 * jax.random.normal(jax.random.fold_in(_gk, 1), (16, 512, 64, 64), jnp.float32)
        return x
    x = _rec_inputs()
    def _L0_conv_setup():
        import jax, jax.numpy as jnp
        import numpy as np
        NUM_STAGES = 3
        EPS = 1e-06

        def _l2norm(x, axis):
            return x / (EPS + jnp.linalg.norm(x, axis=axis, keepdims=True))

        def _l1norm(x, axis):
            return x / (EPS + jnp.sum(x, axis=axis, keepdims=True))
        key = jax.random.key(seed)
        k1, k2 = jax.random.split(key)
        B, C, H, W, K = (16, 512, 64, 64, 64)
        feats = jax.random.normal(k1, (B, C, H, W), dtype=jnp.float32)
        bases = jax.random.normal(k2, (1, C, K), dtype=jnp.float32) * np.sqrt(2.0 / K)
        return {'feats': feats, 'bases': bases}
    _L0_conv_all = _L0_conv_setup()
    _L0_conv_in = {k: v for k, v in _L0_conv_all.items() if k in ('bases', )}
    del _L0_conv_all

    def _L1_conv_setup():
        import jax, jax.numpy as jnp
        import numpy as np
        from jax import lax
        EPS = 1e-05
        DW_THRESH = 4.0
        PW_THRESH = 0.001
        C_IN = 512
        C_OUT = 512

        def _bn(x, g, b, m, v):
            inv = g * lax.rsqrt(v + EPS)
            return x * inv[None, :, None, None] + (b - m * inv)[None, :, None, None]

        def _prune(x, thresh):
            amax = jnp.max(jnp.abs(x), axis=(2, 3), keepdims=True)
            return jnp.where(amax < thresh, jnp.zeros_like(x), x)
        key = jax.random.key(seed)
        ks = jax.random.split(key, 8)
        B, H, W = (64, 28, 28)
        x = jax.random.normal(ks[0], (B, C_IN, H, W), dtype=jnp.float32)
        dw_w = jax.random.normal(ks[1], (C_IN, 1, 3, 3), dtype=jnp.float32) * 0.1
        dw_b = jax.random.normal(ks[2], (C_IN,), dtype=jnp.float32) * 0.1
        bn1_g = jnp.ones((C_IN,), jnp.float32)
        bn1_b = jnp.zeros((C_IN,), jnp.float32)
        bn1_m = jnp.zeros((C_IN,), jnp.float32)
        bn1_v = jnp.ones((C_IN,), jnp.float32)
        pw_w = jax.random.normal(ks[3], (C_OUT, C_IN, 1, 1), dtype=jnp.float32) * 0.05
        pw_b = jax.random.normal(ks[4], (C_OUT,), dtype=jnp.float32) * 0.1
        bn2_g = jnp.ones((C_OUT,), jnp.float32)
        bn2_b = jnp.zeros((C_OUT,), jnp.float32)
        bn2_m = jnp.zeros((C_OUT,), jnp.float32)
        bn2_v = jnp.ones((C_OUT,), jnp.float32)
        return dict(x=x, dw_w=dw_w, dw_b=dw_b, bn1_g=bn1_g, bn1_b=bn1_b, bn1_m=bn1_m, bn1_v=bn1_v, pw_w=pw_w, pw_b=pw_b, bn2_g=bn2_g, bn2_b=bn2_b, bn2_m=bn2_m, bn2_v=bn2_v)
    _L1_conv_all = _L1_conv_setup()
    _L1_conv_in = {k: v for k, v in _L1_conv_all.items() if k in ('dw_w', 'dw_b', 'bn1_g', 'bn1_b', 'bn1_m', 'bn1_v', 'pw_w', 'pw_b', 'bn2_g', 'bn2_b', 'bn2_m', 'bn2_v', )}
    del _L1_conv_all

    return {
        "x": x,
        "L0_conv_bases": _L0_conv_in["bases"],
        "L1_conv_dw_w": _L1_conv_in["dw_w"],
        "L1_conv_dw_b": _L1_conv_in["dw_b"],
        "L1_conv_bn1_g": _L1_conv_in["bn1_g"],
        "L1_conv_bn1_b": _L1_conv_in["bn1_b"],
        "L1_conv_bn1_m": _L1_conv_in["bn1_m"],
        "L1_conv_bn1_v": _L1_conv_in["bn1_v"],
        "L1_conv_pw_w": _L1_conv_in["pw_w"],
        "L1_conv_pw_b": _L1_conv_in["pw_b"],
        "L1_conv_bn2_g": _L1_conv_in["bn2_g"],
        "L1_conv_bn2_b": _L1_conv_in["bn2_b"],
        "L1_conv_bn2_m": _L1_conv_in["bn2_m"],
        "L1_conv_bn2_v": _L1_conv_in["bn2_v"],
    }

def reference(x, L0_conv_bases, L1_conv_dw_w, L1_conv_dw_b, L1_conv_bn1_g, L1_conv_bn1_b, L1_conv_bn1_m, L1_conv_bn1_v, L1_conv_pw_w, L1_conv_pw_b, L1_conv_bn2_g, L1_conv_bn2_b, L1_conv_bn2_m, L1_conv_bn2_v):
    import jax
    import jax.numpy as jnp
    def _L0_conv_ref(feats, bases):
        import jax, jax.numpy as jnp
        import numpy as np
        NUM_STAGES = 3
        EPS = 1e-06

        def _l2norm(x, axis):
            return x / (EPS + jnp.linalg.norm(x, axis=axis, keepdims=True))

        def _l1norm(x, axis):
            return x / (EPS + jnp.sum(x, axis=axis, keepdims=True))
        B, C, H, W = feats.shape
        f = feats.reshape(B, C, H * W)
        b = _l2norm(bases, axis=1)
        b = jnp.broadcast_to(b, (B, C, b.shape[2]))
        attention = None
        for _ in range(NUM_STAGES):
            attention = jnp.einsum('bcn,bck->bnk', f, b)
            attention = jax.nn.softmax(attention, axis=2)
            attention_normed = _l1norm(attention, axis=1)
            b = jnp.einsum('bcn,bnk->bck', f, attention_normed)
            b = _l2norm(b, axis=1)
        b = jax.lax.stop_gradient(b)
        attention = jax.lax.stop_gradient(attention)
        feats_recon = jnp.einsum('bck,bnk->bcn', b, attention)
        return feats_recon.reshape(B, C, H, W)

    def _L1_conv_ref(x, dw_w, dw_b, bn1_g, bn1_b, bn1_m, bn1_v, pw_w, pw_b, bn2_g, bn2_b, bn2_m, bn2_v):
        import jax, jax.numpy as jnp
        import numpy as np
        from jax import lax
        EPS = 1e-05
        DW_THRESH = 4.0
        PW_THRESH = 0.001
        C_IN = 512
        C_OUT = 512

        def _bn(x, g, b, m, v):
            inv = g * lax.rsqrt(v + EPS)
            return x * inv[None, :, None, None] + (b - m * inv)[None, :, None, None]

        def _prune(x, thresh):
            amax = jnp.max(jnp.abs(x), axis=(2, 3), keepdims=True)
            return jnp.where(amax < thresh, jnp.zeros_like(x), x)
        dn = ('NCHW', 'OIHW', 'NCHW')
        h = lax.conv_general_dilated(x, dw_w, window_strides=(1, 1), padding=((1, 1), (1, 1)), feature_group_count=C_IN, dimension_numbers=dn)
        h = h + dw_b[None, :, None, None]
        h = jax.nn.relu(_bn(h, bn1_g, bn1_b, bn1_m, bn1_v))
        h = _prune(h, DW_THRESH)
        h = lax.conv_general_dilated(h, pw_w, window_strides=(1, 1), padding=((0, 0), (0, 0)), dimension_numbers=dn)
        h = h + pw_b[None, :, None, None]
        h = jax.nn.relu(_bn(h, bn2_g, bn2_b, bn2_m, bn2_v))
        h = _prune(h, PW_THRESH)
        return h

    def _gn(v, G=32, eps=1e-5):
        B_, C_, H_, W_ = v.shape
        g = v.reshape(B_, G, C_ // G, H_, W_)
        m = jnp.mean(g, axis=(2, 3, 4), keepdims=True)
        s = jnp.var(g, axis=(2, 3, 4), keepdims=True)
        return ((g - m) / jnp.sqrt(s + eps)).reshape(v.shape)

    def _ln_c(v, eps=1e-6):
        m = jnp.mean(v, axis=1, keepdims=True)
        s = jnp.var(v, axis=1, keepdims=True)
        return (v - m) / jnp.sqrt(s + eps)

    def _ln_t(v, eps=1e-5):
        m = jnp.mean(v, axis=-1, keepdims=True)
        s = jnp.var(v, axis=-1, keepdims=True)
        return (v - m) / jnp.sqrt(s + eps)

    def _to_tokens(v):
        B_, C_, H_, W_ = v.shape
        return v.reshape(B_, C_, H_ * W_).transpose(0, 2, 1)
    def _from_tokens(t, like):
        B_, C_, H_, W_ = like.shape
        return t.transpose(0, 2, 1).reshape(B_, C_, H_, W_)

    x = x + _L0_conv_ref(_gn(x), L0_conv_bases)
    x = x + _L1_conv_ref(_gn(x), L1_conv_dw_w, L1_conv_dw_b, L1_conv_bn1_g, L1_conv_bn1_b, L1_conv_bn1_m, L1_conv_bn1_v, L1_conv_pw_w, L1_conv_pw_b, L1_conv_bn2_g, L1_conv_bn2_b, L1_conv_bn2_m, L1_conv_bn2_v)
    return x


_drawn_inputs = setup_inputs


def setup_inputs(seed=0):
    import zlib

    import numpy as np

    out = dict(_drawn_inputs(seed))
    spreads = {'L1_conv_bn1_g': (1.0, 0.2),
     'L1_conv_bn1_b': (0.0, 0.1),
     'L1_conv_bn1_m': (0.0, 0.1),
     'L1_conv_bn1_v': (1.0, 0.2),
     'L1_conv_bn2_g': (1.0, 0.6),
     'L1_conv_bn2_b': (0.0, 0.1),
     'L1_conv_bn2_m': (0.0, 0.1),
     'L1_conv_bn2_v': (1.0, 0.6)}
    factors = {'L0_conv_bases': 4.246}
    for name, (base, spread) in spreads.items():
        noise = np.random.default_rng([zlib.crc32(name.encode()), seed]).standard_normal(out[name].shape)
        drawn = base * np.exp(spread * noise) if base else spread * noise
        out[name] = jnp.asarray(drawn.astype(out[name].dtype))
    for name, factor in factors.items():
        out[name] = (out[name] * factor).astype(out[name].dtype)
    return out
```

```python
from contextlib import ExitStack

import concourse.bass as bass
from concourse import mybir

F32 = mybir.dt.float32
F16 = mybir.dt.float16
ALU = mybir.AluOpType
ACT = mybir.ActivationFunctionType
AX = mybir.AxisListType

P = 128
GROUP = 16
STAGES = 3
EPS_NORM = 1e-6
EPS_GN = 1e-5
EPS_BN = 1e-5
DW_THRESH = 4.0
PW_THRESH = 0.001
BASE_SCALE = 2.0 ** 10
ATTN_SCALE = 2.0 ** 14
PW_SCALE = 2.0 ** 6
PE_TAPS = 4
ROWS = 16
MM = 512


def conv_preact_block(
    nc, x, bases, dw_w, dw_b, bn1_g, bn1_b, bn1_m, bn1_v, pw_w, pw_b, bn2_g, bn2_b, bn2_m, bn2_v, out,
):
    B, C, HH, WW = x.shape
    K = bases.shape[2]
    N = HH * WW
    T = C // P
    NT = N // P
    GRP = MM // K
    NG = NT // GRP
    NC = N // MM
    NR = HH // ROWS
    CH = ROWS * WW
    LOP = N // 4
    PW = WW + 2
    DVE_TAPS = 9 - PE_TAPS
    INV_N = 1.0 / N
    EV_OWNER = ['a' if e < 8 or e % 2 else 'v' for e in range(NT)]
    EV_DVE = EV_OWNER.count('v')
    EV_NTH = [EV_OWNER[:e + 1].count(EV_OWNER[e]) for e in range(NT)]
    assert C == 512 and K == 64 and CH == 2 * MM and T == 4

    xv = x.rearrange("b (t p) h w -> b t p (h w)", p=P)
    ov = out.rearrange("b (t p) h w -> b t p (h w)", p=P)
    w_dram = nc.dram_tensor("pw_split", [P, T * 2 * C], F16, kind="Internal").ap()

    with ExitStack() as ctx:
        def sb(name, shape, dt):
            return ctx.enter_context(nc.sbuf_tensor(name, shape, dt))

        step_of = {}

        def sem(name, per, unit=1):
            s = ctx.enter_context(nc.semaphore(name))
            step_of[s] = (per, unit)
            return s

        def nth(s, batch, k):
            per, unit = step_of[s]
            return batch * (per * unit) + k * unit

        feat = sb("feat", [P, T, N], F32)
        feat16 = feat[:].rearrange("p t n -> p (t n)").bitcast(F16).rearrange("p (t s n) -> p t s n", t=T, s=2)
        pix = sb("pix", [P, NT * 2 * C], F16)
        featT = pix[:].rearrange("p (i s c) -> p i s c", s=2, c=C)
        hid = pix[:].rearrange("p (j t s m) -> p j t s m", t=T, s=2, m=MM)
        stage = sb("stage", [P, N], F32)
        pad = sb("pad", [P, (HH + 2) * PW], F32)
        img = pad[:].rearrange("p (h w) -> p h w", w=PW)
        att = sb("att", [P, N], F32)
        att16 = att[:].bitcast(F16)
        a_hl = att16[:, 0:N].rearrange("p (i s k) -> p i s k", s=2, k=K)
        aT = att16[:, N:2 * N].rearrange("p (i n) -> p i n", n=P)
        pix32 = pix[:].bitcast(F32).rearrange("p (j t m) -> p j t m", t=T, m=MM)
        x_st = [stage[:], stage[:], stage[:], pad[:, 0:N]]
        res = [pad[:, 0:N], att[:, :]]
        w16 = sb("w16", [P, T, 2, C], F16)
        diag = sb("diag", [P, 2, PE_TAPS, P], F32)
        upd = diag[:].rearrange("p a b c -> p (a b c)")[:, 0:C]
        base = diag[:].rearrange("p a b c -> p (a b c)")[:, C:2 * C]
        work = sb("work", [P, 4, MM], F32)
        logit = [work[:, i, :].rearrange("p (i k) -> p i k", k=K) for i in range(2)]
        attn = [work[:, 2 + i, :].rearrange("p (i k) -> p i k", k=K) for i in range(2)]
        h32 = [work[:, 2 * i:2 * i + 2, :] for i in range(2)]
        bT = sb("bT", [P, 2, C], F16)
        b_hl = sb("b_hl", [P, T, 2, K], F16)
        b0_hl = sb("b0_hl", [P, T, 2, K], F16)
        ident = sb("ident", [P, P], F32)
        ident16 = sb("ident16", [P, P], F16)
        fold = sb("fold", [P, P], F32)
        gavg = sb("gavg", [P, P], F32)
        onesf, scaled, prm_rows = pad[:, 0:P], pad[:, P:2 * P], pad[0:10 * T, 2 * P:3 * P]
        ones16 = sb("ones16", [P, 1], F16)
        small = sb("small", [P, 96], F32)
        col = lambda i, n=1: small[:, i:i + n]
        half_c, mhalf_c = col(0), col(1)
        bn_s = sb("bn_s", [P, NC, 6], F32)
        mv, dev, gm, var_a, s_a, nb_a = col(2, 2), col(4), col(5, 2), col(7), col(8), col(9)
        mx, sm, ri = col(12, GRP), col(20, GRP), col(28, GRP)
        s_col, n2, rt, den = col(36), col(37), col(38), col(39)
        sums, sm1, nmg, sq, var_c, s_c, nb_c = col(40, NC), col(48), col(49), col(50), col(51), col(52), col(53)
        hmx, hm1 = col(54, NR), col(58)
        mask1 = col(60, T)
        rmx, rm1, mask2 = col(64, NR), col(68), col(69)
        prm = sb("prm", [P, 10, T], F32)
        DWB, G1, B1, M1, V1, PWB, G2, B2, M2, V2 = range(10)
        taps = sb("taps", [P, T, 9], F32)
        c1 = sb("c1", [P, T], F32)
        i2 = sb("i2", [P, T], F32)
        c2 = sb("c2", [P, T], F32)

        banks = ctx.enter_context(nc.psum_tensor("banks", [P, 8, MM], F32))
        lg_ps = [banks[:, g, :].rearrange("p (i k) -> p i k", k=K) for g in range(4)]
        dw_ps = [banks[:, 2 * i:2 * i + 2, :].rearrange("p a (h w) -> p (a h) w", w=WW) for i in range(2)]
        mm_ps = [banks[:, 4 + i, :] for i in range(2)]
        up_ps = banks[:, 6, :]
        up_t = banks[:, 6, 0:T * K].rearrange("p (t k) -> p t k", k=K)
        tr_ps = [banks[:, 4 + i, :].bitcast(F16) for i in range(3)]
        pw_ps = [banks[:, i, :] for i in range(4)]
        sum_ps = banks[:, 7, 0:1]
        st_ps = banks[:, 7, 0:2]
        sd_ps = banks[:, 7, 2:3]

        prm_in = sem("prm_in", 1, 16)
        w_in = sem("w_in", 1, 16)
        bas_in = sem("bas_in", 1, 16)
        const_ok = sem("const_ok", 1)
        setup_p = sem("setup_p", 1)
        setup_v = sem("setup_v", 1)
        setup_a = sem("setup_a", 1)
        setup_t = sem("setup_t", 1)
        w_saved = sem("w_saved", 1, 16)
        gate = ctx.enter_context(nc.semaphore("gate"))
        x_in = sem("x_in", T - 1, 16)
        x3_in = sem("x3_in", 1, 16)
        a_stat = sem("a_stat", T)
        a_gm = sem("a_gm", T)
        a_dev = sem("a_dev", T)
        a_gv = sem("a_gv", T)
        a_var = sem("a_var", T)
        a_pow = sem("a_pow", T)
        a_nb = sem("a_nb", T)
        a_norm = sem("a_norm", T)
        a_hi = sem("a_hi", T)
        a_lov = sem("a_lov", T)
        a_lop = sem("a_lop", T)
        bns_ok = sem("bns_ok", T)
        gmc_ok = sem("gmc_ok", T)
        dif_ok = sem("dif_ok", T)
        trx_ok = sem("trx_ok", NT)
        evv_ok = sem("evv_ok", EV_DVE)
        eva_ok = sem("eva_ok", NT - EV_DVE)
        lg_ok = sem("lg_ok", STAGES * NG)
        sub_ok = sem("sub_ok", STAGES * NG)
        exp_ok = sem("exp_ok", STAGES * NG)
        att_ok = sem("att_ok", STAGES * NG)
        ahi_ok = sem("ahi_ok", STAGES * NG)
        alo_ok = sem("alo_ok", STAGES * NG)
        max_ok = sem("max_ok", STAGES * NG)
        sm_ok = sem("sm_ok", STAGES * NG)
        ri_ok = sem("ri_ok", STAGES * NG)
        den_ok = sem("den_ok", STAGES * 3)
        up_ok = sem("up_ok", STAGES)
        upc_ok = sem("upc_ok", STAGES)
        fold_ok = sem("fold_ok", STAGES)
        n2_ok = sem("n2_ok", STAGES)
        rt_ok = sem("rt_ok", STAGES)
        base_ok = sem("base_ok", STAGES)
        bt_ok = sem("bt_ok", STAGES - 1)
        bhi_ok = sem("bhi_ok", STAGES)
        blo_ok = sem("blo_ok", STAGES)
        tra_ok = sem("tra_ok", NG)
        aT_ok = sem("aT_ok", NG)
        xr_in = sem("xr_in", T, 16)
        rec_ok = sem("rec_ok", T * NC)
        x1_ok = sem("x1_ok", T * NC)
        c_sum = sem("c_sum", T)
        c_gm = sem("c_gm", T)
        c_nmg = sem("c_nmg", T)
        c_sq = sem("c_sq", T)
        c_gv = sem("c_gv", T)
        c_var = sem("c_var", T)
        c_pow = sem("c_pow", T)
        c_nb = sem("c_nb", T)
        brd_ok = sem("brd_ok", 1)
        wl_in = sem("wl_in", 1, 16)
        diag_ok = sem("diag_ok", T)
        img_ok = sem("img_ok", T * NR)
        dwp_ok = sem("dwp_ok", T * NR)
        tap_ok = sem("tap_ok", T * NR * DVE_TAPS)
        dwm_ok = sem("dwm_ok", T * NR)
        h32_ok = sem("h32_ok", T * NR)
        hhi_ok = sem("hhi_ok", T * NR)
        hlo_ok = sem("hlo_ok", T * NR)
        hmax_ok = sem("hmax_ok", T)
        mask1_ok = sem("mask1_ok", T)
        w_ok = sem("w_ok", T)
        pw_ok = sem("pw_ok", T * NC)
        r_ok = sem("r_ok", T * NC)
        rmx_ok = sem("rmx_ok", T * NR)
        rmax_ok = sem("rmax_ok", T)
        mask2_ok = sem("mask2_ok", T)
        y_ok = sem("y_ok", T)
        y_out = [sem(f"y_out{i}", T // 2, 16) for i in range(2)]

        SETUP_V = 13 + 4 * T

        block = ctx.enter_context(nc.Block())

        @block.sync
        def _(sp):
            def load_x(batch, t):
                if t in (1, 2):
                    sp.wait_ge(a_lov, nth(a_lov, batch, t))
                    sp.wait_ge(a_lop, nth(a_lop, batch, t))
                sp.dma_start(x_st[t], xv[bass.ds(batch, 1), t].rearrange("a p n -> (a p) n")).then_inc(
                    x_in if t < T - 1 else x3_in, 16)

            def body(b, last):
                for t in range(T):
                    if t == 0:
                        sp.wait_ge(a_lov, nth(a_lov, b, T - 1))
                        sp.wait_ge(a_lop, nth(a_lop, b, T - 1))
                    else:
                        sp.wait_ge(x1_ok, nth(x1_ok, b, t * NC))
                    sp.dma_start(stage[:], xv[bass.ds(b, 1), t].rearrange("a p n -> (a p) n")).then_inc(xr_in, 16)
                    if t == 0:
                        sp.dma_start(w16[:].rearrange("p t s c -> p (t s c)"), w_dram).then_inc(wl_in, 16)
                if not last:
                    sp.wait_ge(x1_ok, nth(x1_ok, b, T * NC))
                    load_x(b + 1, 0)
                for u in range(T):
                    sp.wait_ge(y_ok, nth(y_ok, b, u + 1))
                    sp.dma_start(ov[bass.ds(b, 1), u].rearrange("a p n -> (a p) n"),
                                 res[u % 2]).then_inc(y_out[u % 2], 16)
                    if not last and u < 2:
                        load_x(b + 1, u + 1)
                    if not last and u == 2:
                        sp.wait_ge(y_out[0], nth(y_out[0], b, 2))
                        load_x(b + 1, 3)

            for i, a in enumerate((dw_b, bn1_g, bn1_b, bn1_m, bn1_v, pw_b, bn2_g, bn2_b, bn2_m, bn2_v)):
                sp.dma_start(prm_rows[i * T:(i + 1) * T, :], a.rearrange("(t p) -> t p", p=P)).then_inc(prm_in, 16)
            sp.dma_start(taps[:], dw_w.rearrange("(t p) o h w -> p t (o h w)", p=P)).then_inc(prm_in, 16)
            sp.dma_start(stage[:, 0:T * C].rearrange("p (u c) -> p u c", u=T),
                         pw_w.rearrange("(u p) c h w -> p u (c h w)", p=P)).then_inc(w_in, 16)
            sp.dma_start(work[:, 0, 0:T * K].rearrange("p (t k) -> p t k", t=T),
                         bases.rearrange("o (t p) k -> p t (o k)", p=P)).then_inc(bas_in, 16)
            sp.wait_ge(setup_v, SETUP_V)
            sp.dma_start(w_dram, w16[:].rearrange("p t s c -> p (t s c)")).then_inc(w_saved, 16)
            sp.wait_ge(setup_t, 2 + T)
            for t in range(T):
                load_x(0, t)
            with sp.Fori(0, B - 1) as b:
                body(b, False)
            body(B - 1, True)
            for i in range(2):
                sp.wait_ge(y_out[i], nth(y_out[i], B, 0))

        @block.gpsimd
        def _(pool):
            def lo_a(batch, t):
                pool.wait_ge(a_hi, nth(a_hi, batch, t + 1))
                pool.tensor_tensor(feat16[:, t, 1, 0:LOP], x_st[t][:, 0:LOP],
                                   feat16[:, t, 0, 0:LOP], ALU.subtract).then_inc(a_lop, 1)

            def pow_a(batch, t):
                pool.wait_ge(a_var, nth(a_var, batch, t + 1))
                pool.tensor_tensor(s_a, var_a, mhalf_c, ALU.pow).then_inc(a_pow, 1)

            def body(b, last):
                pow_a(b, T - 1)
                lo_a(b, T - 1)
                for s in range(STAGES):
                    for g in range(NG):
                        n = s * NG + g
                        pool.wait_ge(ahi_ok, nth(ahi_ok, b, n + 1))
                        pool.tensor_tensor(a_hl[:, g * GRP:(g + 1) * GRP, 1, :], attn[g % 2],
                                                     a_hl[:, g * GRP:(g + 1) * GRP, 0, :], ALU.subtract).then_inc(alo_ok, 1)
                    pool.wait_ge(n2_ok, nth(n2_ok, b, s + 1))
                    pool.tensor_tensor(rt, n2, half_c, ALU.pow).then_inc(rt_ok, 1)
                pool.wait_ge(a_lov, nth(a_lov, b, T))
                pool.sem_inc(gate, 1)
                pool.memset(pad[:], 0.0).then_inc(brd_ok, 1)

                def pow_c(t):
                    pool.wait_ge(c_var, nth(c_var, b, t + 1))
                    pool.tensor_tensor(s_c, var_c, mhalf_c, ALU.pow).then_inc(c_pow, 1)

                pow_c(0)
                for t in range(T):
                    for j in range(NR):
                        n = t * NR + j
                        if j == 2 and t + 1 < T:
                            pow_c(t + 1)
                        pool.wait_ge(hhi_ok, nth(hhi_ok, b, n + 1))
                        pool.tensor_tensor(hid[:, 2 * j:2 * j + 2, t, 1, :], h32[n % 2],
                                                     hid[:, 2 * j:2 * j + 2, t, 0, :], ALU.subtract).then_inc(hlo_ok, 1)
                if not last:
                    for t in range(T - 1):
                        pow_a(b + 1, t)
                        lo_a(b + 1, t)

            pool.memset(ident[:], 0.0)
            pool.memset(ident16[:], 0.0)
            pool.memset(fold[:], 0.0)
            pool.memset(gavg[:], 1.0 / GROUP)
            pool.memset(ones16[:], 1.0)
            pool.memset(onesf, 1.0)
            pool.memset(scaled, 0.0)
            pool.memset(half_c, 0.5)
            pool.memset(mhalf_c, -0.5).then_inc(setup_p, 1)
            pool.wait_ge(setup_p, 1)
            pool.affine_select(out=ident[:], in_=ident[:], compare_op=ALU.not_equal, fill=1.0, base=0,
                               pattern=[[-1, P]], channel_multiplier=1)
            pool.affine_select(out=scaled, in_=scaled, compare_op=ALU.not_equal, fill=PW_SCALE, base=0,
                               pattern=[[-1, P]], channel_multiplier=1)
            pool.affine_select(out=ident16[:], in_=ident16[:], compare_op=ALU.not_equal, fill=1.0, base=0,
                               pattern=[[-1, P]], channel_multiplier=1)
            fv = fold[:].rearrange("p (a k) -> p a k", a=2)
            pool.affine_select(out=fv, in_=fv, compare_op=ALU.not_equal, fill=1.0, base=0,
                               pattern=[[0, 2], [-1, K]], channel_multiplier=1)
            gv = gavg[:].rearrange("p (a k) -> p a k", k=GROUP)
            pool.affine_select(out=gv, in_=gv, compare_op=ALU.is_ge, fill=0.0, base=0,
                               pattern=[[-GROUP, P // GROUP], [0, GROUP]], channel_multiplier=1).then_inc(setup_p, 1)
            pool.wait_ge(setup_p, 2)
            pool.affine_select(out=fv, in_=fv, compare_op=ALU.not_equal, fill=1.0, base=-K,
                               pattern=[[0, 2], [-1, K]], channel_multiplier=1)
            pool.affine_select(out=gv, in_=gv, compare_op=ALU.is_ge, fill=0.0, base=GROUP - 1,
                               pattern=[[GROUP, P // GROUP], [0, GROUP]], channel_multiplier=-1).then_inc(const_ok, 1)
            pool.wait_ge(setup_v, 3)
            pool.tensor_tensor(prm[:, V1, :], prm[:, V1, :], mhalf_c.to_broadcast([P, T]), ALU.pow)
            pool.tensor_tensor(prm[:, V2, :], prm[:, V2, :], mhalf_c.to_broadcast([P, T]), ALU.pow).then_inc(setup_p, 1)
            pool.wait_ge(setup_v, 11)
            pool.tensor_tensor(work[:, 1, 0:K], work[:, 1, 0:K], half_c.to_broadcast([P, K]), ALU.pow).then_inc(setup_p, 1)
            for t in range(T - 1):
                pow_a(0, t)
                lo_a(0, t)
            with pool.Fori(0, B - 1) as b:
                body(b, False)
            body(B - 1, True)

        @block.scalar
        def _(act):
            def hi_a(batch, t, b_free):
                act.wait_ge(a_norm, nth(a_norm, batch, t + 1))
                if b_free is not None:
                    act.wait_ge(y_ok, nth(y_ok, b_free, t + 1))
                act.activation(feat16[:, t, 0, :], x_st[t], ACT.Identity).then_inc(a_hi, 1)

            def squares(b, t):
                act.wait_ge(c_nmg, nth(c_nmg, b, t + 1))
                act.activation(pix32[:, :, t, :], feat[:, t, :].rearrange("p (j m) -> p j m", m=MM),
                               ACT.Square, bias=nmg, accum_out=sq).then_inc(c_sq, 1)

            def image(b, t, j):
                if j == 0:
                    act.wait_ge(c_nb, nth(c_nb, b, t + 1))
                    if t == 0:
                        act.wait_ge(brd_ok, nth(brd_ok, b, 1))
                if t > 0:
                    act.wait_ge(dwm_ok, nth(dwm_ok, b, (t - 1) * NR + min(j + 2, NR)))
                act.activation(img[:, 1 + j * ROWS:1 + (j + 1) * ROWS, 1:1 + WW],
                                         feat[:, t, j * CH:(j + 1) * CH].rearrange("p (h w) -> p h w", w=WW),
                                         ACT.Identity, bias=nb_c, scale=s_c).then_inc(img_ok, 1)

            def diagonals(b, t):
                if t > 1:
                    act.wait_ge(dwp_ok, nth(dwp_ok, b, (t - 1) * NR))
                for k in range(PE_TAPS):
                    ins = act.activation(diag[:, t % 2, k, :], ident[:], ACT.Identity, scale=taps[:, t, k:k + 1])
                ins.then_inc(diag_ok, 1)

            def hidden(b, t, j):
                n = t * NR + j
                act.wait_ge(dwm_ok, nth(dwm_ok, b, n + 1))
                if n >= 2:
                    act.wait_ge(hlo_ok, nth(hlo_ok, b, n - 1))
                hv = h32[n % 2].rearrange("p a (h w) -> p (a h) w", w=WW)
                act.activation(hv, dw_ps[n % 2], ACT.Relu, bias=c1[:, t:t + 1]).then_inc(h32_ok, 1)
                act.wait_ge(h32_ok, nth(h32_ok, b, n + 1))
                act.activation(hid[:, 2 * j:2 * j + 2, t, 0, :], h32[n % 2], ACT.Identity).then_inc(hhi_ok, 1)

            def result(b, u, j):
                n = u * NC + j
                act.wait_ge(pw_ok, nth(pw_ok, b, n + 1))
                if j == 0:
                    if u >= 2:
                        act.wait_ge(y_out[u % 2], nth(y_out[u % 2], b, u // 2))
                act.activation(res[u % 2][:, j * MM:(j + 1) * MM], pw_ps[n % 4], ACT.Relu,
                                       bias=c2[:, u:u + 1], scale=i2[:, u:u + 1]).then_inc(r_ok, 1)

            def take_block(b, e):
                act.wait_ge(trx_ok, nth(trx_ok, b, e + 1))
                act.activation(featT[:, 4 * (e % 8):4 * (e % 8) + 4, :, (e // 8) * P:(e // 8 + 1) * P],
                               tr_ps[e % 3].rearrange("p (i s c) -> p i s c", s=2, c=P),
                               ACT.Identity).then_inc(eva_ok, 1)

            def body(b, last):
                mine = [e for e in range(NT) if EV_OWNER[e] == 'a']
                for e in mine[0:11]:
                    take_block(b, e)
                hi_a(b, T - 1, None)
                for e in mine[11:16]:
                    take_block(b, e)
                for s in range(STAGES):
                    for g in range(NG + 1):
                        if s == 0 and g == 1:
                            for e in mine[16:]:
                                take_block(b, e)
                        if g < NG:
                            n = s * NG + g
                            act.wait_ge(sub_ok, nth(sub_ok, b, n + 1))
                            act.activation(logit[g % 2], logit[g % 2], ACT.Exp, scale=1.0 / BASE_SCALE).then_inc(exp_ok, 1)
                        if g >= 1:
                            n = s * NG + g - 1
                            act.wait_ge(att_ok, nth(att_ok, b, n + 1))
                            if g == 1 and s > 0:
                                act.wait_ge(up_ok, nth(up_ok, b, s))
                            act.activation(a_hl[:, (g - 1) * GRP:g * GRP, 0, :], attn[(g - 1) % 2],
                                                     ACT.Identity).then_inc(ahi_ok, 1)
                    if s == STAGES - 1:
                        for g in range(NG):
                            act.wait_ge(tra_ok, nth(tra_ok, b, g + 1))
                            act.activation(aT[:, g * GRP:(g + 1) * GRP, :],
                                           tr_ps[g % 2].rearrange("p (i n) -> p i n", n=P),
                                           ACT.Identity).then_inc(aT_ok, 1)
                    act.wait_ge(up_ok, nth(up_ok, b, s + 1))
                    act.activation(s_col, sum_ps, ACT.Identity)
                    act.activation(upd, up_ps, ACT.Identity).then_inc(upc_ok, 1)
                    act.wait_ge(fold_ok, nth(fold_ok, b, s + 1))
                    act.wait_ge(upc_ok, nth(upc_ok, b, s + 1))
                    act.activation(upd, up_ps, ACT.Square, accum_out=n2).then_inc(n2_ok, 1)
                    if s < STAGES - 1:
                        act.wait_ge(bt_ok, nth(bt_ok, b, s + 1))
                        act.activation(b_hl[:, :, 0, :], up_t, ACT.Identity).then_inc(bhi_ok, 1)
                    else:
                        act.wait_ge(base_ok, nth(base_ok, b, s + 1))
                        act.activation(bT[:, 0, :], base, ACT.Identity).then_inc(bhi_ok, 1)
                squares(b, 0)
                act.wait_ge(blo_ok, nth(blo_ok, b, STAGES))
                diagonals(b, 0)
                for j in range(NR):
                    image(b, 0, j)
                for t in range(T):
                    hidden(b, t, 0)
                    hidden(b, t, 1)
                    if t + 1 < T:
                        squares(b, t + 1)
                        diagonals(b, t + 1)
                    hidden(b, t, 2)
                    if t + 1 < T:
                        image(b, t + 1, 0)
                        image(b, t + 1, 1)
                    hidden(b, t, 3)
                    if t + 1 < T:
                        image(b, t + 1, 2)
                        image(b, t + 1, 3)
                for u in range(T):
                    for j in range(NC):
                        result(b, u, j)
                        if not last and (u, j) in ((1, 2), (2, 5), (3, 7)):
                            hi_a(b + 1, u - 1, b)
                if not last:
                    act.wait_ge(y_ok, nth(y_ok, b, T))
                    act.wait_ge(y_out[1], nth(y_out[1], b + 1, 0))

            for t in range(T):
                for h in range(1):
                    act.wait_ge(setup_t, 3 + t)
                    act.activation(w16[:, t, 0, :], banks[:, t, :], ACT.Identity).then_inc(setup_a, 1)
            for t in range(T - 1):
                hi_a(0, t, None)
            with act.Fori(0, B - 1) as b:
                body(b, False)
            body(B - 1, True)

        @block.vector
        def _(dve):
            def stats_a(batch, t):
                if t < T - 1:
                    dve.wait_ge(x_in, nth(x_in, batch, t + 1))
                else:
                    dve.wait_ge(x3_in, nth(x3_in, batch, 1))
                for j in range(NC):
                    ins = dve.bn_stats(bn_s[:, j, :], x_st[t][:, j * MM:(j + 1) * MM])
                ins.then_inc(bns_ok, 1)
                dve.wait_ge(bns_ok, nth(bns_ok, batch, t + 1))
                dve.sem_inc(gate, 1)
                dve.bn_aggr(mv, bn_s[:].rearrange("p j s -> p (j s)")).then_inc(a_stat, 1)

            def spread_a(batch, t):
                dve.wait_ge(a_gm, nth(a_gm, batch, t + 1))
                dve.tensor_copy(gm, st_ps).then_inc(gmc_ok, 1)
                dve.wait_ge(gmc_ok, nth(gmc_ok, batch, t + 1))
                dve.tensor_tensor(dev, mv[:, 0:1], gm[:, 0:1], ALU.subtract).then_inc(dif_ok, 1)
                dve.wait_ge(dif_ok, nth(dif_ok, batch, t + 1))
                dve.tensor_tensor(dev, dev, dev, ALU.mult).then_inc(a_dev, 1)

            def scale_a(batch, t):
                dve.wait_ge(a_gv, nth(a_gv, batch, t + 1))
                dve.tensor_scalar(var_a, sd_ps, gm[:, 1:2], EPS_GN, ALU.add, ALU.add).then_inc(a_var, 1)
                dve.wait_ge(a_pow, nth(a_pow, batch, t + 1))
                dve.scalar_tensor_tensor(nb_a, gm[:, 0:1], -1.0, s_a, ALU.mult, ALU.mult).then_inc(a_nb, 1)
                dve.wait_ge(a_nb, nth(a_nb, batch, t + 1))
                dve.tensor_scalar(x_st[t], x_st[t], s_a, nb_a, ALU.mult, ALU.add).then_inc(a_norm, 1)

            def low_a(batch, t):
                dve.wait_ge(a_hi, nth(a_hi, batch, t + 1))
                dve.tensor_tensor(feat16[:, t, 1, LOP:N], x_st[t][:, LOP:N],
                                  feat16[:, t, 0, LOP:N], ALU.subtract).then_inc(a_lov, 1)

            def take_block(b, e):
                dve.wait_ge(trx_ok, nth(trx_ok, b, e + 1))
                dve.tensor_copy(featT[:, 4 * (e % 8):4 * (e % 8) + 4, :, (e // 8) * P:(e // 8 + 1) * P],
                                tr_ps[e % 3].rearrange("p (i s c) -> p i s c", s=2, c=P)).then_inc(evv_ok, 1)

            def softmax(b, n, g):
                dve.wait_ge(lg_ok, nth(lg_ok, b, n + 1))
                if n > 0:
                    dve.wait_ge(sub_ok, nth(sub_ok, b, n))
                dve.tensor_reduce(mx, lg_ps[g], AX.X, ALU.max).then_inc(max_ok, 1)
                dve.wait_ge(max_ok, nth(max_ok, b, n + 1))
                dve.tensor_tensor(logit[g % 2], lg_ps[g],
                                            mx.unsqueeze(2).to_broadcast([P, GRP, K]), ALU.subtract).then_inc(sub_ok, 1)

            def normalise(b, n, g):
                dve.wait_ge(exp_ok, nth(exp_ok, b, n + 1))
                if n > 0:
                    dve.wait_ge(att_ok, nth(att_ok, b, n))
                dve.tensor_reduce(sm, logit[g % 2], AX.X, ALU.add).then_inc(sm_ok, 1)
                dve.wait_ge(sm_ok, nth(sm_ok, b, n + 1))
                dve.reciprocal(ri, sm).then_inc(ri_ok, 1)
                dve.wait_ge(ri_ok, nth(ri_ok, b, n + 1))
                if n >= 2:
                    dve.wait_ge(alo_ok, nth(alo_ok, b, n - 1))
                dve.scalar_tensor_tensor(attn[g % 2], logit[g % 2], ATTN_SCALE,
                                                   ri.unsqueeze(2).to_broadcast([P, GRP, K]), ALU.mult, ALU.mult).then_inc(att_ok, 1)

            def rebase(b, s):
                dve.wait_ge(fold_ok, nth(fold_ok, b, s + 1))
                dve.tensor_scalar(den, sum_ps, EPS_NORM * ATTN_SCALE, EPS_NORM, ALU.add, ALU.mult).then_inc(den_ok, 1)
                dve.wait_ge(den_ok, nth(den_ok, b, 3 * s + 1))
                dve.wait_ge(rt_ok, nth(rt_ok, b, s + 1))
                dve.tensor_tensor(den, den, rt, ALU.add).then_inc(den_ok, 1)
                dve.wait_ge(den_ok, nth(den_ok, b, 3 * s + 2))
                dve.reciprocal(den, den).then_inc(den_ok, 1)
                dve.wait_ge(den_ok, nth(den_ok, b, 3 * s + 3))
                dve.tensor_scalar(base, up_ps, den, BASE_SCALE, ALU.mult, ALU.mult).then_inc(base_ok, 1)
                if s < STAGES - 1:
                    dve.wait_ge(bhi_ok, nth(bhi_ok, b, s + 1))
                    dve.tensor_tensor(b_hl[:, :, 1, :], up_t, b_hl[:, :, 0, :], ALU.subtract).then_inc(blo_ok, 1)
                else:
                    dve.wait_ge(bhi_ok, nth(bhi_ok, b, s + 1))
                    dve.tensor_tensor(bT[:, 1, :], base, bT[:, 0, :], ALU.subtract).then_inc(blo_ok, 1)

            def add_x(b, t):
                dve.wait_ge(xr_in, nth(xr_in, b, t + 1))
                for j in range(NC):
                    dve.wait_ge(rec_ok, nth(rec_ok, b, t * NC + j + 1))
                    dve.scalar_tensor_tensor(
                        feat[:, t, j * MM:(j + 1) * MM], mm_ps[j % 2], 1.0 / (BASE_SCALE * ATTN_SCALE),
                        stage[:, j * MM:(j + 1) * MM], ALU.mult, ALU.add, accum_out=sums[:, j:j + 1]).then_inc(x1_ok, 1)
                dve.wait_ge(x1_ok, nth(x1_ok, b, (t + 1) * NC))
                dve.tensor_reduce(sm1, sums, AX.X, ALU.add).then_inc(c_sum, 1)

            def mean_c(b, t):
                dve.wait_ge(c_gm, nth(c_gm, b, t + 1))
                dve.tensor_scalar(nmg, st_ps[:, 0:1], -INV_N, None, ALU.mult).then_inc(c_nmg, 1)

            def scale_c(b, t):
                dve.wait_ge(c_gv, nth(c_gv, b, t + 1))
                dve.tensor_scalar(var_c, sd_ps, INV_N, EPS_GN, ALU.mult, ALU.add).then_inc(c_var, 1)
                dve.wait_ge(c_pow, nth(c_pow, b, t + 1))
                dve.tensor_tensor(nb_c, nmg, s_c, ALU.mult).then_inc(c_nb, 1)

            def depthwise(b, t, j):
                n = t * NR + j
                dve.wait_ge(dwp_ok, nth(dwp_ok, b, n + 1))
                for i, k in enumerate(range(PE_TAPS, 9)):
                    dy, dx = k // 3, k % 3
                    dve.scalar_tensor_tensor(
                        dw_ps[n % 2], img[:, j * ROWS + dy:(j + 1) * ROWS + dy, dx:dx + WW],
                        taps[:, t, k:k + 1], dw_ps[n % 2], ALU.mult, ALU.add).then_inc(tap_ok, 1)
                    dve.wait_ge(tap_ok, nth(tap_ok, b, n * DVE_TAPS + i + 1))
                dve.tensor_reduce(hmx[:, j:j + 1], dw_ps[n % 2], AX.XY, ALU.max).then_inc(dwm_ok, 1)

            def prune(b, t):
                dve.wait_ge(dwm_ok, nth(dwm_ok, b, (t + 1) * NR))
                dve.tensor_reduce(hm1, hmx, AX.X, ALU.max).then_inc(hmax_ok, 1)
                dve.wait_ge(hmax_ok, nth(hmax_ok, b, t + 1))
                dve.tensor_scalar(mask1[:, t:t + 1], hm1, c1[:, t:t + 1], DW_THRESH, ALU.add, ALU.is_ge).then_inc(mask1_ok, 1)
                dve.wait_ge(mask1_ok, nth(mask1_ok, b, t + 1))
                if t == 0:
                    dve.wait_ge(wl_in, nth(wl_in, b, 1))
                dve.tensor_scalar(w16[:, t], w16[:, t], mask1[:, t:t + 1], None, ALU.mult).then_inc(w_ok, 1)

            def maxima(b, u, j):
                dve.wait_ge(r_ok, nth(r_ok, b, u * NC + 2 * j + 2))
                dve.tensor_reduce(rmx[:, j:j + 1], res[u % 2][:, j * CH:(j + 1) * CH], AX.X, ALU.max).then_inc(rmx_ok, 1)

            def finish(b, u):
                dve.wait_ge(rmx_ok, nth(rmx_ok, b, (u + 1) * NR))
                dve.tensor_reduce(rm1, rmx, AX.X, ALU.max).then_inc(rmax_ok, 1)
                dve.wait_ge(rmax_ok, nth(rmax_ok, b, u + 1))
                dve.tensor_scalar(mask2, rm1, PW_THRESH, None, ALU.is_ge).then_inc(mask2_ok, 1)
                dve.wait_ge(mask2_ok, nth(mask2_ok, b, u + 1))
                dve.scalar_tensor_tensor(res[u % 2], res[u % 2], mask2, feat[:, u, :], ALU.mult, ALU.add).then_inc(y_ok, 1)

            def body(b, last):
                mine = [e for e in range(NT) if EV_OWNER[e] == 'v']
                low_a(b, T - 2)
                stats_a(b, T - 1)
                take_block(b, mine[0])
                take_block(b, mine[1])
                spread_a(b, T - 1)
                take_block(b, mine[2])
                take_block(b, mine[3])
                scale_a(b, T - 1)
                for e in mine[4:8]:
                    take_block(b, e)
                low_a(b, T - 1)
                for s in range(STAGES):
                    for g in range(NG + 1):
                        if s == 0 and g == 1:
                            for e in mine[8:]:
                                take_block(b, e)
                        if g < NG:
                            softmax(b, s * NG + g, g)
                        if g >= 1:
                            normalise(b, s * NG + g - 1, g - 1)
                    rebase(b, s)
                add_x(b, 0)
                mean_c(b, 0)
                scale_c(b, 0)
                for t in range(T):
                    depthwise(b, t, 0)
                    if t + 1 < T:
                        add_x(b, t + 1)
                    depthwise(b, t, 1)
                    if t + 1 < T:
                        mean_c(b, t + 1)
                    depthwise(b, t, 2)
                    if t + 1 < T:
                        scale_c(b, t + 1)
                    depthwise(b, t, 3)
                    prune(b, t)
                for u in range(T):
                    for j in range(NR):
                        if not last:
                            if (u, j) == (0, 0):
                                stats_a(b + 1, 0)
                            if (u, j) == (0, 2):
                                spread_a(b + 1, 0)
                            if (u, j) == (0, 3):
                                scale_a(b + 1, 0)
                            if (u, j) == (1, 2):
                                low_a(b + 1, 0)
                            if (u, j) == (1, 3):
                                stats_a(b + 1, 1)
                            if (u, j) == (2, 2):
                                scale_a(b + 1, 1)
                            if (u, j) == (2, 3):
                                low_a(b + 1, 1)
                            if (u, j) == (3, 2):
                                spread_a(b + 1, 2)
                            if (u, j) == (3, 3):
                                scale_a(b + 1, 2)
                        maxima(b, u, j)
                    finish(b, u)
                    if not last and u == 1:
                        spread_a(b + 1, 1)
                    if not last and u == 2:
                        stats_a(b + 1, 2)

            n = [0]

            def step(ins):
                n[0] += 1
                ins.then_inc(setup_v, 1)
                dve.wait_ge(setup_v, n[0])

            dve.wait_ge(setup_t, 1)
            step(dve.tensor_copy(prm[:], banks[:, 7, 0:10 * T].rearrange("p (i t) -> p i t", t=T)))
            step(dve.tensor_scalar(prm[:, V1, :], prm[:, V1, :], EPS_BN, None, ALU.add))
            step(dve.tensor_scalar(prm[:, V2, :], prm[:, V2, :], EPS_BN, None, ALU.add))
            dve.wait_ge(setup_p, 3)
            step(dve.tensor_tensor(prm[:, G1, :], prm[:, G1, :], prm[:, V1, :], ALU.mult))
            step(dve.tensor_tensor(prm[:, G2, :], prm[:, G2, :], prm[:, V2, :], ALU.mult))
            step(dve.tensor_tensor(prm[:, DWB:DWB + 1, :], prm[:, DWB:DWB + 1, :], prm[:, M1:M1 + 1, :], ALU.subtract))
            step(dve.tensor_tensor(prm[:, PWB, :], prm[:, PWB, :], prm[:, M2, :], ALU.subtract))
            step(dve.tensor_tensor(prm[:, DWB, :], prm[:, DWB, :], prm[:, G1, :], ALU.mult))
            step(dve.tensor_tensor(prm[:, PWB, :], prm[:, PWB, :], prm[:, G2, :], ALU.mult))
            dve.wait_ge(bas_in, 16)
            step(dve.tensor_tensor(work[:, 2, 0:T * K], work[:, 0, 0:T * K], work[:, 0, 0:T * K], ALU.mult))
            dve.wait_ge(setup_t, 2)
            step(dve.tensor_copy(work[:, 1, 0:K], up_ps[:, 0:K]))
            dve.wait_ge(setup_p, 4)
            step(dve.tensor_scalar(work[:, 1, 0:K], work[:, 1, 0:K], EPS_NORM, None, ALU.add))
            step(dve.reciprocal(work[:, 1, 0:K], work[:, 1, 0:K]))
            for t in range(T):
                step(dve.scalar_tensor_tensor(work[:, 0, t * K:(t + 1) * K], work[:, 0, t * K:(t + 1) * K],
                                              BASE_SCALE, work[:, 1, 0:K], ALU.mult, ALU.mult))
                step(dve.tensor_copy(b0_hl[:, t, 0, :], work[:, 0, t * K:(t + 1) * K]))
                dve.tensor_tensor(b0_hl[:, t, 1, :], work[:, 0, t * K:(t + 1) * K], b0_hl[:, t, 0, :], ALU.subtract)
                dve.wait_ge(setup_a, t + 1)
                step(dve.tensor_tensor(w16[:, t, 1, :], banks[:, t, :], w16[:, t, 0, :], ALU.subtract))
                step(dve.tensor_scalar(taps[:, t, :], taps[:, t, :], prm[:, G1, t:t + 1], None, ALU.mult))
            assert n[0] == SETUP_V, n[0]
            dve.tensor_tensor(c1[:], prm[:, DWB, :], prm[:, B1, :], ALU.add)
            dve.tensor_tensor(c2[:], prm[:, PWB, :], prm[:, B2, :], ALU.add)
            dve.tensor_scalar(i2[:], prm[:, G2, :], 1.0 / PW_SCALE, None, ALU.mult).then_inc(setup_v, 1)
            for t in range(T - 1):
                stats_a(0, t)
                spread_a(0, t)
                scale_a(0, t)
                if t < T - 2:
                    low_a(0, t)
            with dve.Fori(0, B - 1) as b:
                body(b, False)
            body(B - 1, True)

        @block.tensor
        def _(pe):
            mm = nc.tensor.matmul

            def stat_a(batch, t):
                pe.wait_ge(a_stat, nth(a_stat, batch, t + 1))
                mm(st_ps, gavg[:], mv, start=True, stop=True).then_inc(a_gm, 1)

            def spread_a(batch, t):
                pe.wait_ge(a_dev, nth(a_dev, batch, t + 1))
                mm(sd_ps, gavg[:], dev, start=True, stop=True).then_inc(a_gv, 1)

            def logits(bh, g, tiles):
                for i in range(GRP):
                    nt = g * GRP + i
                    px = slice(nt * P, (nt + 1) * P)
                    for t in tiles:
                        for fs, bs in ((0, 0), (0, 1), (1, 0)):
                            ins = mm(lg_ps[g][:, i, :], feat16[:, t, fs, px], bh[:, t, bs, :],
                                     start=(i == 0 and t == 0 and fs + bs == 0),
                                     stop=(t == T - 1 and fs == 1), skip_group_check=True)
                return ins

            def turn_block(b, e):
                if e >= 3:
                    own, ev = (evv_ok, EV_NTH[e - 3]) if EV_OWNER[e - 3] == 'v' else (eva_ok, EV_NTH[e - 3])
                    pe.wait_ge(own, nth(own, b, ev))
                pe.sem_inc(gate, 1)
                t, blk = e // 8, e % 8
                out_v = tr_ps[e % 3].rearrange("p (i s c) -> p i s c", s=2, c=P)
                for i in range(4):
                    for fs in range(2):
                        px = slice((4 * blk + i) * P, (4 * blk + i + 1) * P)
                        ins = nc.tensor.transpose(out_v[:, i, fs, :], feat16[:, t, fs, px], ident16[:])
                ins.then_inc(trx_ok, 1)

            def turn_attn(b, g):
                pe.wait_ge(alo_ok, nth(alo_ok, b, (STAGES - 1) * NG + g + 1))
                if g >= 2:
                    pe.wait_ge(aT_ok, nth(aT_ok, b, g - 1))
                pe.sem_inc(gate, 1)
                for i in range(GRP):
                    ins = nc.tensor.transpose(tr_ps[g % 2][:, i * P:(i + 1) * P],
                                              a_hl[:, g * GRP + i].rearrange("p s k -> p (s k)"), ident16[:])
                ins.then_inc(tra_ok, 1)

            def update(b, s, g):
                for i in range(GRP):
                    nt = g * GRP + i
                    first, end = nt == 0, nt == NT - 1
                    mm(up_ps, a_hl[:, nt].rearrange("p s k -> p (s k)"), featT[:, nt, 0, :],
                       start=first, stop=False, skip_group_check=True)
                    mm(sum_ps, a_hl[:, nt].rearrange("p s k -> p (s k)"), ones16[:],
                       start=first, stop=end, skip_group_check=True)
                    ins = mm(up_ps[0:K], a_hl[:, nt, 0, :], featT[:, nt, 1, :],
                             start=False, stop=end, skip_group_check=True)
                return ins

            def recon(b, t):
                for j in range(NC):
                    n = t * NC + j
                    if n >= 2:
                        pe.wait_ge(x1_ok, nth(x1_ok, b, n - 1))
                    mm(mm_ps[j % 2], bT[:, 0, t * P:(t + 1) * P], aT[:, 4 * j:4 * j + 4, :],
                       start=True, stop=False)
                    mm(mm_ps[j % 2], bT[0:K, 1, t * P:(t + 1) * P], aT[0:K, 4 * j:4 * j + 4, :],
                                 start=False, stop=True).then_inc(rec_ok, 1)

            def depthwise(b, t, j):
                n = t * NR + j
                pe.wait_ge(img_ok, nth(img_ok, b, t * NR + min(j + 2, NR)))
                if j == 0:
                    pe.wait_ge(diag_ok, nth(diag_ok, b, t + 1))
                if n >= 2:
                    pe.wait_ge(h32_ok, nth(h32_ok, b, n - 1))
                for h in range(2):
                    o = banks[:, 2 * (n % 2) + h, :].rearrange("p (h w) -> p h w", w=WW)
                    for k in range(PE_TAPS):
                        r = j * ROWS + h * ROWS // 2 + k // 3
                        ins = mm(o, diag[:, t % 2, k, :], img[:, r:r + ROWS // 2, k % 3:k % 3 + WW],
                                 start=(k == 0), stop=(k == PE_TAPS - 1))
                ins.then_inc(dwp_ok, 1)

            def pointwise(b, u, j):
                n = u * NC + j
                if n >= 4:
                    pe.wait_ge(r_ok, nth(r_ok, b, n - 3))
                else:
                    pe.wait_ge(h32_ok, nth(h32_ok, b, T * NR - 1 + n // 2))
                if u == 0:
                    pe.wait_ge(hlo_ok, nth(hlo_ok, b, (T - 1) * NR + j // 2 + 1))
                for t in range(T):
                    if n == 0:
                        pe.wait_ge(w_ok, nth(w_ok, b, t + 1))
                    for ws, hs in ((0, 0), (0, 1), (1, 0)):
                        ins = mm(pw_ps[n % 4], w16[:, t, ws, u * P:(u + 1) * P], hid[:, j, t, hs, :],
                                 start=(t == 0 and ws + hs == 0), stop=(t == T - 1 and ws == 1))
                ins.then_inc(pw_ok, 1)

            def body(b, last):
                for s in range(STAGES):
                    if s == 0:
                        for g in range(NG):
                            logits(b0_hl, g, [0, 1])
                        for e in range(0, 8):
                            turn_block(b, e)
                        stat_a(b, T - 1)
                        for e in range(8, 12):
                            turn_block(b, e)
                        spread_a(b, T - 1)
                        for e in range(12, 16):
                            turn_block(b, e)
                        pe.wait_ge(a_lov, nth(a_lov, b, T - 1))
                        pe.wait_ge(a_lop, nth(a_lop, b, T - 1))
                        for g in range(NG):
                            logits(b0_hl, g, [2])
                        for e in range(16, 24):
                            turn_block(b, e)
                        pe.wait_ge(a_lov, nth(a_lov, b, T))
                        pe.wait_ge(a_lop, nth(a_lop, b, T))
                        for g in range(NG):
                            logits(b0_hl, g, [T - 1]).then_inc(lg_ok, 1)
                        for e in range(24, NT):
                            turn_block(b, e)
                        pe.wait_ge(evv_ok, nth(evv_ok, b, EV_DVE))
                        pe.wait_ge(eva_ok, nth(eva_ok, b, NT - EV_DVE))
                    else:
                        pe.wait_ge(blo_ok, nth(blo_ok, b, s))
                        for g in range(NG):
                            logits(b_hl, g, range(T)).then_inc(lg_ok, 1)
                    for g in range(NG):
                        pe.wait_ge(alo_ok, nth(alo_ok, b, s * NG + g + 1))
                        ins = update(b, s, g)
                    ins.then_inc(up_ok, 1)
                    if s == STAGES - 1:
                        for g in range(NG):
                            turn_attn(b, g)
                    pe.wait_ge(upc_ok, nth(upc_ok, b, s + 1))
                    mm(sum_ps, fold[:], s_col, start=True, stop=True)
                    mm(up_ps, fold[:], upd, start=True, stop=True).then_inc(fold_ok, 1)
                    if s < STAGES - 1:
                        pe.wait_ge(base_ok, nth(base_ok, b, s + 1))
                        pe.wait_ge(n2_ok, nth(n2_ok, b, s + 1))
                        pe.sem_inc(gate, 1)
                        for t in range(T):
                            ins = nc.tensor.transpose(up_t[:, t, :], base[0:K, t * P:(t + 1) * P], ident[0:K, 0:K])
                        ins.then_inc(bt_ok, 1)
                pe.wait_ge(blo_ok, nth(blo_ok, b, STAGES))
                pe.wait_ge(aT_ok, nth(aT_ok, b, NG))

                def mean_c(t):
                    pe.wait_ge(c_sum, nth(c_sum, b, t + 1))
                    mm(st_ps[:, 0:1], gavg[:], sm1, start=True, stop=True).then_inc(c_gm, 1)

                def var_c_(t):
                    pe.wait_ge(c_sq, nth(c_sq, b, t + 1))
                    mm(sd_ps, gavg[:], sq, start=True, stop=True).then_inc(c_gv, 1)

                recon(b, 0)
                mean_c(0)
                var_c_(0)
                for t in range(T):
                    depthwise(b, t, 0)
                    depthwise(b, t, 1)
                    if t + 1 < T:
                        recon(b, t + 1)
                    depthwise(b, t, 2)
                    if t + 1 < T:
                        mean_c(t + 1)
                    depthwise(b, t, 3)
                    if t + 1 < T:
                        var_c_(t + 1)
                for u in range(T):
                    for j in range(NC):
                        pointwise(b, u, j)
                        if not last:
                            if (u, j) == (0, 2):
                                stat_a(b + 1, 0)
                            if (u, j) == (0, 4):
                                spread_a(b + 1, 0)
                            if (u, j) == (1, 7):
                                stat_a(b + 1, 1)
                            if (u, j) == (2, 3):
                                spread_a(b + 1, 1)
                            if (u, j) == (3, 4):
                                stat_a(b + 1, 2)
                            if (u, j) == (3, 5):
                                spread_a(b + 1, 2)
                if not last:
                    pe.wait_ge(r_ok, nth(r_ok, b, T * NC))

            pe.wait_ge(const_ok, 1)
            pe.wait_ge(prm_in, 16 * 11)
            nc.tensor.transpose(banks[:, 7, 0:10 * T], prm_rows, ident[0:10 * T, 0:10 * T]).then_inc(setup_t, 1)
            pe.wait_ge(setup_v, 10)
            for t in range(T):
                ins = mm(up_ps[:, 0:K], onesf, work[:, 2, t * K:(t + 1) * K], start=(t == 0), stop=(t == T - 1))
            ins.then_inc(setup_t, 1)
            pe.wait_ge(w_in, 16)
            for t in range(T):
                for u in range(T):
                    ins = mm(banks[:, t, u * P:(u + 1) * P], stage[:, u * C + t * P:u * C + (t + 1) * P], scaled,
                             start=True, stop=True)
                ins.then_inc(setup_t, 1)
            for t in range(T - 1):
                stat_a(0, t)
                spread_a(0, t)
            with pe.Fori(0, B - 1) as b:
                body(b, False)
            body(B - 1, True)


_INS = ['x', 'L0_conv_bases', 'L1_conv_dw_w', 'L1_conv_dw_b', 'L1_conv_bn1_g', 'L1_conv_bn1_b', 'L1_conv_bn1_m',
        'L1_conv_bn1_v', 'L1_conv_pw_w', 'L1_conv_pw_b', 'L1_conv_bn2_g', 'L1_conv_bn2_b', 'L1_conv_bn2_m',
        'L1_conv_bn2_v']


def kernel(**inputs):
    import numpy as _np
    import concourse.bacc as _bacc
    from concourse import mybir as _mybir
    from concourse.bass_utils import run_bass_kernel_spmd as _run

    nc = _bacc.Bacc("TRN2", target_bir_lowering=False, num_devices=1)
    arrays, args = {}, []
    for name in _INS:
        a = _np.ascontiguousarray(inputs[name])
        arrays[f"in_{name}_dram"] = a
        args.append(nc.dram_tensor(f"in_{name}_dram", a.shape, _mybir.dt.from_np(a.dtype), kind="ExternalInput").ap())
    shape = inputs['x'].shape
    args.append(nc.dram_tensor("out_0_dram", shape, _mybir.dt.float32, kind="ExternalOutput").ap())
    conv_preact_block(nc, *args)
    r = _run(nc, [arrays], core_ids=[0])
    return r.results[0]["out_0_dram"]
```

```python
from contextlib import ExitStack

import numpy as np

import concourse.bass as bass
from concourse import mybir

F32 = mybir.dt.float32
F16 = mybir.dt.float16
ALU = mybir.AluOpType
ACT = mybir.ActivationFunctionType
AX = mybir.AxisListType

P = 128
GROUP = 16
STAGES = 3
EPS_NORM = 1e-6
EPS_GN = 1e-5
EPS_BN = 1e-5
DW_THRESH = 4.0
PW_THRESH = 0.001
BASE_SCALE = 2.0 ** 10
ATTN_SCALE = 2.0 ** 14
PW_SCALE = 2.0 ** 6
PE_TAPS = 4
ROWS = 16
MM = 512


def below(x):
    return float(np.nextafter(np.float32(x), np.float32(0.0)))


def conv_preact_block(
    nc, x, bases, dw_w, dw_b, bn1_g, bn1_b, bn1_m, bn1_v, pw_w, pw_b, bn2_g, bn2_b, bn2_m, bn2_v, out,
):
    B, C, HH, WW = x.shape
    K = bases.shape[2]
    N = HH * WW
    T = C // P
    NT = N // P
    GRP = MM // K
    NG = NT // GRP
    NC = N // MM
    NR = HH // ROWS
    CH = ROWS * WW
    LOP = N // 4
    PW = WW + 2
    DVE_TAPS = 9 - PE_TAPS
    INV_N = 1.0 / N
    BLOCKS = [(i % 2, i // 2) for i in range(NT // 2)] + [(t, i) for t in (2, 3) for i in range(NT // 4)]
    EARLY = NT // 2
    EV_OWNER = ['v' if (e in (0, 2, 4) if e < EARLY else e % 2 == 0) else 'a' for e in range(NT)]
    EV_DVE = EV_OWNER.count('v')
    EV_NTH = [EV_OWNER[:e + 1].count(EV_OWNER[e]) for e in range(NT)]
    assert C == 512 and K == 64 and CH == 2 * MM and T == 4

    xv = x.rearrange("b (t p) h w -> b t p (h w)", p=P)
    ov = out.rearrange("b (t p) h w -> b t p (h w)", p=P)
    w_dram = nc.dram_tensor("pw_split", [P, T * 2 * C], F16, kind="Internal").ap()

    with ExitStack() as ctx:
        def sb(name, shape, dt):
            return ctx.enter_context(nc.sbuf_tensor(name, shape, dt))

        step_of = {}

        def sem(name, per, unit=1):
            s = ctx.enter_context(nc.semaphore(name))
            step_of[s] = (per, unit)
            return s

        def nth(s, batch, k):
            per, unit = step_of[s]
            return batch * (per * unit) + k * unit

        feat = sb("feat", [P, T, N], F32)
        feat16 = feat[:].rearrange("p t n -> p (t n)").bitcast(F16).rearrange("p (t s n) -> p t s n", t=T, s=2)
        pix = sb("pix", [P, NT * 2 * C], F16)
        featT = pix[:].rearrange("p (i s c) -> p i s c", s=2, c=C)
        hid = pix[:].rearrange("p (j t s m) -> p j t s m", t=T, s=2, m=MM)
        stage = sb("stage", [P, N], F32)
        pad = sb("pad", [P, (HH + 2) * PW], F32)
        img = pad[:].rearrange("p (h w) -> p h w", w=PW)
        att = sb("att", [P, N], F32)
        att16 = att[:].bitcast(F16)
        a_hl = att16[:, 0:N].rearrange("p (i s k) -> p i s k", s=2, k=K)
        aT = att16[:, N:2 * N].rearrange("p (i n) -> p i n", n=P)
        pix32 = pix[:].bitcast(F32).rearrange("p (j t m) -> p j t m", t=T, m=MM)
        x_st = [stage[:], stage[:], stage[:], pad[:, 0:N]]
        res = [pad[:, 0:N], att[:, :]]
        w16 = sb("w16", [P, T, 2, C], F16)
        diag = sb("diag", [P, 2, PE_TAPS, P], F32)
        upd = diag[:].rearrange("p a b c -> p (a b c)")[:, 0:C]
        base = diag[:].rearrange("p a b c -> p (a b c)")[:, C:2 * C]
        work = sb("work", [P, 4, MM], F32)
        logit = [work[:, i, :].rearrange("p (i k) -> p i k", k=K) for i in range(2)]
        attn = [work[:, 2 + i, :].rearrange("p (i k) -> p i k", k=K) for i in range(2)]
        h32 = [work[:, 2 * i:2 * i + 2, :] for i in range(2)]
        bT = sb("bT", [P, 2, C], F16)
        b_hl = sb("b_hl", [P, T, 2, K], F16)
        b0_hl = sb("b0_hl", [P, T, 2, K], F16)
        ident = sb("ident", [P, P], F32)
        ident16 = sb("ident16", [P, P], F16)
        fold = sb("fold", [P, P], F32)
        gavg = sb("gavg", [P, P], F32)
        onesf, scaled, prm_rows = pad[:, 0:P], pad[:, P:2 * P], pad[0:10 * T, 2 * P:3 * P]
        asum = sb("asum", [P, NG, K], F32)
        small = sb("small", [P, 180], F32)
        col = lambda i, n=1: small[:, i:i + n]
        half_c, mhalf_c, one_c, dwt_c, pwt_c = col(0), col(1), col(10), col(11), col(36)
        bn_s = sb("bn_s", [P, NC, 6], F32)
        mv, dev, gm, var_a, s_a, nb_a = col(2, 2), col(4), col(5, 2), col(7), col(8), col(9)
        mx, sm, ri = col(12, GRP), col(20, GRP), col(28, GRP)
        n2, rt, den = col(37), col(38), col(39)
        sums, sm1, nmg, sq, var_c, s_c, nb_c = (
            [col(o + i * w, w) for i in range(T)]
            for o, w in ((80, NC), (140, 1), (144, 1), (148, 1), (152, 1), (156, 1), (160, 1)))
        hov = [col(40 + i * NR, NR) for i in range(2)]
        rov = [col(124 + i * NC, NC) for i in range(2)]
        hm1 = col(58)
        mask1 = col(60, T)
        rm1, mask2 = col(68), col(69)
        prm = sb("prm", [P, 10, T], F32)
        DWB, G1, B1, M1, V1, PWB, G2, B2, M2, V2 = range(10)
        taps = sb("taps", [P, T, 9], F32)
        c1 = sb("c1", [P, T], F32)
        i2 = sb("i2", [P, T], F32)
        c2 = sb("c2", [P, T], F32)

        banks = ctx.enter_context(nc.psum_tensor("banks", [P, 8, MM], F32))
        lg_ps = [banks[:, g, :].rearrange("p (i k) -> p i k", k=K) for g in range(4)]
        dw_ps = [banks[:, 2 * i:2 * i + 2, :].rearrange("p a (h w) -> p (a h) w", w=WW) for i in range(3)]
        mm_ps = [banks[:, 4 + i, :] for i in range(2)]
        up_ps = banks[:, 6, :]
        rc_ps = banks[:, 6, :]
        up_t = banks[:, 6, 0:T * K].rearrange("p (t k) -> p t k", k=K)
        tr_ps = [banks[:, 4 + i, :].bitcast(F16) for i in range(3)]
        pw_ps = [banks[:, i, :] for i in (2, 3, 0, 1)]
        sum_ps = banks[:, 7, 0:1]
        st_ps = banks[:, 7, 0:2]
        sd_ps = banks[:, 7, 2:3]

        prm_in = sem("prm_in", 1, 16)
        w_in = sem("w_in", 1, 16)
        bas_in = sem("bas_in", 1, 16)
        const_ok = sem("const_ok", 1)
        setup_p = sem("setup_p", 1)
        setup_v = sem("setup_v", 1)
        setup_a = sem("setup_a", 1)
        setup_t = sem("setup_t", 1)
        w_saved = sem("w_saved", 1, 16)
        gate = ctx.enter_context(nc.semaphore("gate"))
        x_in = sem("x_in", T - 1, 16)
        x3_in = sem("x3_in", 1, 16)
        a_stat = sem("a_stat", T)
        a_gm = sem("a_gm", T)
        a_dev = sem("a_dev", T)
        a_gv = sem("a_gv", T)
        a_var = sem("a_var", T)
        a_pow = sem("a_pow", T)
        a_nb = sem("a_nb", T)
        a_norm = sem("a_norm", T)
        a_hi = sem("a_hi", T)
        a_lov = sem("a_lov", T)
        a_lop = sem("a_lop", T)
        bns_ok = sem("bns_ok", T)
        gmc_ok = sem("gmc_ok", T)
        dif_ok = sem("dif_ok", T)
        trx_ok = sem("trx_ok", NT)
        evv_ok = sem("evv_ok", EV_DVE)
        eva_ok = sem("eva_ok", NT - EV_DVE)
        lg_ok = sem("lg_ok", STAGES * NG)
        sub_ok = sem("sub_ok", STAGES * NG)
        exp_ok = sem("exp_ok", STAGES * NG)
        att_ok = sem("att_ok", STAGES * NG)
        ahi_ok = sem("ahi_ok", STAGES * NG)
        alo_ok = sem("alo_ok", STAGES * NG)
        max_ok = sem("max_ok", STAGES * NG)
        sm_ok = sem("sm_ok", STAGES * NG)
        ri_ok = sem("ri_ok", STAGES * NG)
        den_ok = sem("den_ok", STAGES * 3)
        asum_ok = sem("asum_ok", STAGES * NG)
        ssum_ok = sem("ssum_ok", STAGES)
        up_ok = sem("up_ok", STAGES)
        upc_ok = sem("upc_ok", STAGES)
        fold_ok = sem("fold_ok", STAGES)
        n2_ok = sem("n2_ok", STAGES)
        rt_ok = sem("rt_ok", STAGES)
        base_ok = sem("base_ok", STAGES)
        bt_ok = sem("bt_ok", STAGES - 1)
        bhi_ok = sem("bhi_ok", STAGES)
        blo_ok = sem("blo_ok", STAGES)
        tra_ok = sem("tra_ok", NG)
        aT_ok = sem("aT_ok", NG)
        xr_in = [sem(f"xr_in{i}", T, 16) for i in range(NR)]
        rec_ok = sem("rec_ok", T * NC)
        x1_ok = sem("x1_ok", T * NC)
        c_sum = sem("c_sum", T)
        c_gm = sem("c_gm", T)
        c_nmg = sem("c_nmg", T)
        c_sq = sem("c_sq", T)
        c_gv = sem("c_gv", T)
        c_var = sem("c_var", T)
        c_pow = sem("c_pow", T)
        c_nb = sem("c_nb", T)
        brd_ok = sem("brd_ok", 1)
        wl_in = sem("wl_in", 1, 16)
        diag_ok = sem("diag_ok", T)
        img_ok = sem("img_ok", T * NR)
        dwp_ok = sem("dwp_ok", T * NR)
        tap_ok = sem("tap_ok", T * NR * DVE_TAPS)
        hov_ok = sem("hov_ok", T * NR)
        h32_ok = sem("h32_ok", T * NR)
        hhi_ok = sem("hhi_ok", T * NR)
        hlo_ok = sem("hlo_ok", T * NR)
        hmax_ok = sem("hmax_ok", T)
        mask1_ok = sem("mask1_ok", T)
        w_ok = sem("w_ok", T)
        pw_ok = sem("pw_ok", T * NC)
        r_ok = sem("r_ok", T * NC)
        rov_ok = sem("rov_ok", T * NC)
        rmax_ok = sem("rmax_ok", T)
        mask2_ok = sem("mask2_ok", T)
        y_ok = sem("y_ok", T)
        y_out = [sem(f"y_out{i}", T // 2, 16) for i in range(2)]

        SETUP_V = 13 + 4 * T

        def place_T(e):
            t, i = BLOCKS[e]
            return featT[:, 4 * i:4 * i + 4, :, t * P:(t + 1) * P]

        block = ctx.enter_context(nc.Block())

        @block.sync
        def _(sp):
            def load_x(batch, t):
                if t in (1, 2):
                    sp.wait_ge(a_lov, nth(a_lov, batch, t))
                    sp.wait_ge(a_lop, nth(a_lop, batch, t))
                sp.dma_start(x_st[t], xv[bass.ds(batch, 1), t].rearrange("a p n -> (a p) n")).then_inc(
                    x_in if t < T - 1 else x3_in, 16)

            def body(b, last):
                for t in range(T):
                    for j in range(NR):
                        if t > 0:
                            sp.wait_ge(x1_ok, nth(x1_ok, b, (t - 1) * NC + 2 * j + 2))
                        elif j == 0:
                            sp.wait_ge(a_lov, nth(a_lov, b, T - 1))
                            sp.wait_ge(a_lop, nth(a_lop, b, T - 1))
                        sp.dma_start(stage[:, j * CH:(j + 1) * CH],
                                     xv[bass.ds(b, 1), t, :, j * CH:(j + 1) * CH].rearrange("a p n -> (a p) n")
                                     ).then_inc(xr_in[j], 16)
                    if t == 0:
                        sp.dma_start(w16[:].rearrange("p t s c -> p (t s c)"), w_dram).then_inc(wl_in, 16)
                if not last:
                    sp.wait_ge(x1_ok, nth(x1_ok, b, T * NC))
                    load_x(b + 1, 0)
                for u in range(T):
                    sp.wait_ge(y_ok, nth(y_ok, b, u + 1))
                    sp.dma_start(ov[bass.ds(b, 1), u].rearrange("a p n -> (a p) n"),
                                 res[u % 2]).then_inc(y_out[u % 2], 16)
                    if not last and u < 2:
                        load_x(b + 1, u + 1)
                    if not last and u == 2:
                        sp.wait_ge(y_out[0], nth(y_out[0], b, 2))
                        load_x(b + 1, 3)

            for i, a in enumerate((dw_b, bn1_g, bn1_b, bn1_m, bn1_v, pw_b, bn2_g, bn2_b, bn2_m, bn2_v)):
                sp.dma_start(prm_rows[i * T:(i + 1) * T, :], a.rearrange("(t p) -> t p", p=P)).then_inc(prm_in, 16)
            sp.dma_start(taps[:], dw_w.rearrange("(t p) o h w -> p t (o h w)", p=P)).then_inc(prm_in, 16)
            sp.dma_start(stage[:, 0:T * C].rearrange("p (u c) -> p u c", u=T),
                         pw_w.rearrange("(u p) c h w -> p u (c h w)", p=P)).then_inc(w_in, 16)
            sp.dma_start(work[:, 0, 0:T * K].rearrange("p (t k) -> p t k", t=T),
                         bases.rearrange("o (t p) k -> p t (o k)", p=P)).then_inc(bas_in, 16)
            sp.wait_ge(setup_v, SETUP_V)
            sp.dma_start(w_dram, w16[:].rearrange("p t s c -> p (t s c)")).then_inc(w_saved, 16)
            sp.wait_ge(setup_t, 2 + T)
            for t in range(T):
                load_x(0, t)
            with sp.Fori(0, B - 1) as b:
                body(b, False)
            body(B - 1, True)
            for i in range(2):
                sp.wait_ge(y_out[i], nth(y_out[i], B, 0))

        @block.gpsimd
        def _(pool):
            def lo_a(batch, t):
                pool.wait_ge(a_hi, nth(a_hi, batch, t + 1))
                pool.tensor_tensor(feat16[:, t, 1, 0:LOP], x_st[t][:, 0:LOP],
                                   feat16[:, t, 0, 0:LOP], ALU.subtract).then_inc(a_lop, 1)

            def pow_a(batch, t):
                pool.wait_ge(a_var, nth(a_var, batch, t + 1))
                pool.tensor_tensor(s_a, var_a, mhalf_c, ALU.pow).then_inc(a_pow, 1)

            def body(b, last):
                pow_a(b, T - 1)
                lo_a(b, T - 1)
                for s in range(STAGES):
                    for g in range(NG):
                        n = s * NG + g
                        pool.wait_ge(ahi_ok, nth(ahi_ok, b, n + 1))
                        pool.tensor_tensor(a_hl[:, g * GRP:(g + 1) * GRP, 1, :], attn[g % 2],
                                                     a_hl[:, g * GRP:(g + 1) * GRP, 0, :], ALU.subtract).then_inc(alo_ok, 1)
                    pool.wait_ge(n2_ok, nth(n2_ok, b, s + 1))
                    pool.tensor_tensor(rt, n2, half_c, ALU.pow).then_inc(rt_ok, 1)
                pool.wait_ge(a_lov, nth(a_lov, b, T))
                pool.sem_inc(gate, 1)
                pool.memset(pad[:], 0.0).then_inc(brd_ok, 1)

                def pow_c(t):
                    pool.wait_ge(c_var, nth(c_var, b, t + 1))
                    pool.tensor_tensor(s_c[t], var_c[t], mhalf_c, ALU.pow).then_inc(c_pow, 1)

                pow_c(0)
                pow_c(1)
                for t in range(T):
                    for j in range(NR):
                        n = t * NR + j
                        if j == 3 and t + 2 < T:
                            pow_c(t + 2)
                        pool.wait_ge(hhi_ok, nth(hhi_ok, b, n + 1))
                        pool.tensor_tensor(hid[:, 2 * j:2 * j + 2, t, 1, :], h32[n % 2],
                                                     hid[:, 2 * j:2 * j + 2, t, 0, :], ALU.subtract).then_inc(hlo_ok, 1)
                if not last:
                    for t in range(T - 1):
                        pow_a(b + 1, t)
                        lo_a(b + 1, t)

            pool.memset(ident[:], 0.0)
            pool.memset(ident16[:], 0.0)
            pool.memset(fold[:], 0.0)
            pool.memset(gavg[:], 1.0 / GROUP)
            pool.memset(one_c, 1.0)
            pool.memset(dwt_c, -below(DW_THRESH))
            pool.memset(pwt_c, -below(PW_THRESH))
            pool.memset(onesf, 1.0)
            pool.memset(scaled, 0.0)
            pool.memset(half_c, 0.5)
            pool.memset(mhalf_c, -0.5).then_inc(setup_p, 1)
            pool.wait_ge(setup_p, 1)
            pool.affine_select(out=ident[:], in_=ident[:], compare_op=ALU.not_equal, fill=1.0, base=0,
                               pattern=[[-1, P]], channel_multiplier=1)
            pool.affine_select(out=scaled, in_=scaled, compare_op=ALU.not_equal, fill=PW_SCALE, base=0,
                               pattern=[[-1, P]], channel_multiplier=1)
            pool.affine_select(out=ident16[:], in_=ident16[:], compare_op=ALU.not_equal, fill=1.0, base=0,
                               pattern=[[-1, P]], channel_multiplier=1)
            fv = fold[:].rearrange("p (a k) -> p a k", a=2)
            pool.affine_select(out=fv, in_=fv, compare_op=ALU.not_equal, fill=1.0, base=0,
                               pattern=[[0, 2], [-1, K]], channel_multiplier=1)
            gv = gavg[:].rearrange("p (a k) -> p a k", k=GROUP)
            pool.affine_select(out=gv, in_=gv, compare_op=ALU.is_ge, fill=0.0, base=0,
                               pattern=[[-GROUP, P // GROUP], [0, GROUP]], channel_multiplier=1).then_inc(setup_p, 1)
            pool.wait_ge(setup_p, 2)
            pool.affine_select(out=fv, in_=fv, compare_op=ALU.not_equal, fill=1.0, base=-K,
                               pattern=[[0, 2], [-1, K]], channel_multiplier=1)
            pool.affine_select(out=gv, in_=gv, compare_op=ALU.is_ge, fill=0.0, base=GROUP - 1,
                               pattern=[[GROUP, P // GROUP], [0, GROUP]], channel_multiplier=-1).then_inc(const_ok, 1)
            pool.wait_ge(setup_v, 3)
            pool.tensor_tensor(prm[:, V1, :], prm[:, V1, :], mhalf_c.to_broadcast([P, T]), ALU.pow)
            pool.tensor_tensor(prm[:, V2, :], prm[:, V2, :], mhalf_c.to_broadcast([P, T]), ALU.pow).then_inc(setup_p, 1)
            pool.wait_ge(setup_v, 11)
            pool.tensor_tensor(work[:, 1, 0:K], work[:, 1, 0:K], half_c.to_broadcast([P, K]), ALU.pow).then_inc(setup_p, 1)
            for t in range(T - 1):
                pow_a(0, t)
                lo_a(0, t)
            with pool.Fori(0, B - 1) as b:
                body(b, False)
            body(B - 1, True)

        @block.scalar
        def _(act):
            def hi_a(batch, t, b_free):
                act.wait_ge(a_norm, nth(a_norm, batch, t + 1))
                if b_free is not None:
                    act.wait_ge(y_ok, nth(y_ok, b_free, t + 1))
                act.activation(feat16[:, t, 0, :], x_st[t], ACT.Identity).then_inc(a_hi, 1)

            def squares(b, t):
                act.wait_ge(c_nmg, nth(c_nmg, b, t + 1))
                act.activation(pix32[:, :, t, :], feat[:, t, :].rearrange("p (j m) -> p j m", m=MM),
                               ACT.Square, bias=nmg[t], accum_out=sq[t]).then_inc(c_sq, 1)

            def image(b, t, j):
                if j == 0:
                    act.wait_ge(c_nb, nth(c_nb, b, t + 1))
                    if t == 0:
                        act.wait_ge(brd_ok, nth(brd_ok, b, 1))
                if t > 0:
                    act.wait_ge(tap_ok, nth(tap_ok, b, ((t - 1) * NR + min(j + 2, NR)) * DVE_TAPS))
                act.activation(img[:, 1 + j * ROWS:1 + (j + 1) * ROWS, 1:1 + WW],
                                         feat[:, t, j * CH:(j + 1) * CH].rearrange("p (h w) -> p h w", w=WW),
                                         ACT.Identity, bias=nb_c[t], scale=s_c[t]).then_inc(img_ok, 1)

            def diagonals(b, t):
                if t > 1:
                    act.wait_ge(dwp_ok, nth(dwp_ok, b, (t - 1) * NR))
                for k in range(PE_TAPS):
                    ins = act.activation(diag[:, t % 2, k, :], ident[:], ACT.Identity, scale=taps[:, t, k:k + 1])
                ins.then_inc(diag_ok, 1)

            def hidden(b, t, j):
                n = t * NR + j
                if t + 1 < T and j > 0:
                    image(b, t + 1, j - 1)
                act.wait_ge(tap_ok, nth(tap_ok, b, (n + 1) * DVE_TAPS))
                if n >= 2:
                    act.wait_ge(hlo_ok, nth(hlo_ok, b, n - 1))
                hv = h32[n % 2].rearrange("p a (h w) -> p (a h) w", w=WW)
                act.activation(hv, dw_ps[n % 3], ACT.Relu, bias=c1[:, t:t + 1]).then_inc(h32_ok, 1)
                if t + 1 < T and j == NR - 1:
                    image(b, t + 1, j)
                act.wait_ge(h32_ok, nth(h32_ok, b, n + 1))
                if t >= 2 and j == 0:
                    act.wait_ge(hmax_ok, nth(hmax_ok, b, t - 1))
                act.activation(hid[:, 2 * j:2 * j + 2, t, 1, :], h32[n % 2], ACT.Relu, bias=dwt_c,
                               accum_out=hov[t % 2][:, j:j + 1]).then_inc(hov_ok, 1)
                act.activation(hid[:, 2 * j:2 * j + 2, t, 0, :], h32[n % 2], ACT.Identity).then_inc(hhi_ok, 1)

            def result(b, u, j):
                n = u * NC + j
                act.wait_ge(pw_ok, nth(pw_ok, b, n + 1))
                if j == 0:
                    if u >= 2:
                        act.wait_ge(y_out[u % 2], nth(y_out[u % 2], b, u // 2))
                act.activation(res[u % 2][:, j * MM:(j + 1) * MM], pw_ps[n % 4], ACT.Relu,
                                       bias=c2[:, u:u + 1], scale=i2[:, u:u + 1]).then_inc(r_ok, 1)

            def over(b, u, j):
                n = u * NC + j
                act.wait_ge(r_ok, nth(r_ok, b, n + 1))
                if n >= 4:
                    act.wait_ge(rov_ok, nth(rov_ok, b, n - 3))
                else:
                    act.wait_ge(hlo_ok, nth(hlo_ok, b, T * NR - 1 + n // 2))
                if u >= 2 and j == 0:
                    act.wait_ge(rmax_ok, nth(rmax_ok, b, u - 1))
                act.activation(work[:, n % 4, :], res[u % 2][:, j * MM:(j + 1) * MM], ACT.Relu, bias=pwt_c,
                               accum_out=rov[u % 2][:, j:j + 1]).then_inc(rov_ok, 1)

            def take_block(b, e):
                act.wait_ge(trx_ok, nth(trx_ok, b, e + 1))
                act.activation(place_T(e),
                               tr_ps[e % 3].rearrange("p (i s c) -> p i s c", s=2, c=P),
                               ACT.Identity).then_inc(eva_ok, 1)

            def body(b, last):
                mine = [e for e in range(EARLY, NT) if EV_OWNER[e] == 'a']
                hi_a(b, T - 1, None)
                for e in mine[0:4]:
                    take_block(b, e)
                for s in range(STAGES):
                    for g in range(NG + 1):
                        if s == 0 and g == 1:
                            for e in mine[4:]:
                                take_block(b, e)
                        if g < NG:
                            n = s * NG + g
                            act.wait_ge(sub_ok, nth(sub_ok, b, n + 1))
                            act.activation(logit[g % 2], logit[g % 2], ACT.Exp, scale=1.0 / BASE_SCALE).then_inc(exp_ok, 1)
                        if g >= 1:
                            n = s * NG + g - 1
                            act.wait_ge(att_ok, nth(att_ok, b, n + 1))
                            if g == 1 and s > 0:
                                act.wait_ge(up_ok, nth(up_ok, b, s))
                            act.activation(a_hl[:, (g - 1) * GRP:g * GRP, 0, :], attn[(g - 1) % 2],
                                                     ACT.Identity).then_inc(ahi_ok, 1)
                    if s == STAGES - 1:
                        for g in range(NG):
                            act.wait_ge(tra_ok, nth(tra_ok, b, g + 1))
                            act.activation(aT[:, g * GRP:(g + 1) * GRP, :],
                                           tr_ps[g % 2].rearrange("p (i n) -> p i n", n=P),
                                           ACT.Identity).then_inc(aT_ok, 1)
                    act.wait_ge(up_ok, nth(up_ok, b, s + 1))
                    act.activation(upd, up_ps, ACT.Identity).then_inc(upc_ok, 1)
                    act.wait_ge(fold_ok, nth(fold_ok, b, s + 1))
                    act.wait_ge(upc_ok, nth(upc_ok, b, s + 1))
                    act.activation(upd, up_ps, ACT.Square, accum_out=n2).then_inc(n2_ok, 1)
                    if s < STAGES - 1:
                        act.wait_ge(bt_ok, nth(bt_ok, b, s + 1))
                        act.activation(b_hl[:, :, 0, :], up_t, ACT.Identity).then_inc(bhi_ok, 1)
                    else:
                        act.wait_ge(base_ok, nth(base_ok, b, s + 1))
                        act.activation(bT[:, 0, :], base, ACT.Identity).then_inc(bhi_ok, 1)
                squares(b, 0)
                act.wait_ge(blo_ok, nth(blo_ok, b, STAGES))
                diagonals(b, 0)
                for j in range(NR):
                    image(b, 0, j)
                squares(b, 1)
                for t in range(T):
                    for j in range(NR):
                        hidden(b, t, j)
                        if j == 0 and t + 1 < T:
                            diagonals(b, t + 1)
                        if j == 2 and t + 2 < T:
                            squares(b, t + 2)
                for u in range(T):
                    for j in range(NC):
                        result(b, u, j)
                        if j > 0:
                            over(b, u, j - 1)
                        if not last and (u, j) in ((1, 2), (2, 6), (3, 7)):
                            hi_a(b + 1, u - 1, b)
                        if not last and u == T - 1:
                            for e in (2 * j - 2, 2 * j - 1):
                                if e >= 0 and EV_OWNER[e] == 'a':
                                    take_block(b + 1, e)
                    over(b, u, NC - 1)
                if not last:
                    take_block(b + 1, EARLY - 2)
                    take_block(b + 1, EARLY - 1)
                    act.wait_ge(y_ok, nth(y_ok, b, T))
                    act.wait_ge(y_out[1], nth(y_out[1], b + 1, 0))

            for t in range(T):
                for h in range(1):
                    act.wait_ge(setup_t, 3 + t)
                    act.activation(w16[:, t, 0, :], banks[:, t, :], ACT.Identity).then_inc(setup_a, 1)
            for t in range(T - 1):
                hi_a(0, t, None)
            for e in range(EARLY):
                if EV_OWNER[e] == 'a':
                    take_block(0, e)
            with act.Fori(0, B - 1) as b:
                body(b, False)
            body(B - 1, True)

        @block.vector
        def _(dve):
            def stats_a(batch, t):
                if t < T - 1:
                    dve.wait_ge(x_in, nth(x_in, batch, t + 1))
                else:
                    dve.wait_ge(x3_in, nth(x3_in, batch, 1))
                for j in range(NC):
                    ins = dve.bn_stats(bn_s[:, j, :], x_st[t][:, j * MM:(j + 1) * MM])
                ins.then_inc(bns_ok, 1)
                dve.wait_ge(bns_ok, nth(bns_ok, batch, t + 1))
                dve.sem_inc(gate, 1)
                dve.bn_aggr(mv, bn_s[:].rearrange("p j s -> p (j s)")).then_inc(a_stat, 1)

            def spread_a(batch, t):
                dve.wait_ge(a_gm, nth(a_gm, batch, t + 1))
                dve.tensor_copy(gm, st_ps).then_inc(gmc_ok, 1)
                dve.wait_ge(gmc_ok, nth(gmc_ok, batch, t + 1))
                dve.tensor_tensor(dev, mv[:, 0:1], gm[:, 0:1], ALU.subtract).then_inc(dif_ok, 1)
                dve.wait_ge(dif_ok, nth(dif_ok, batch, t + 1))
                dve.tensor_tensor(dev, dev, dev, ALU.mult).then_inc(a_dev, 1)

            def scale_a(batch, t):
                dve.wait_ge(a_gv, nth(a_gv, batch, t + 1))
                dve.tensor_scalar(var_a, sd_ps, gm[:, 1:2], EPS_GN, ALU.add, ALU.add).then_inc(a_var, 1)
                dve.wait_ge(a_pow, nth(a_pow, batch, t + 1))
                dve.scalar_tensor_tensor(nb_a, gm[:, 0:1], -1.0, s_a, ALU.mult, ALU.mult).then_inc(a_nb, 1)
                dve.wait_ge(a_nb, nth(a_nb, batch, t + 1))
                dve.tensor_scalar(x_st[t], x_st[t], s_a, nb_a, ALU.mult, ALU.add).then_inc(a_norm, 1)

            def low_a(batch, t):
                dve.wait_ge(a_hi, nth(a_hi, batch, t + 1))
                dve.tensor_tensor(feat16[:, t, 1, LOP:N], x_st[t][:, LOP:N],
                                  feat16[:, t, 0, LOP:N], ALU.subtract).then_inc(a_lov, 1)

            def take_block(b, e):
                dve.wait_ge(trx_ok, nth(trx_ok, b, e + 1))
                dve.tensor_copy(place_T(e),
                                tr_ps[e % 3].rearrange("p (i s c) -> p i s c", s=2, c=P)).then_inc(evv_ok, 1)

            def softmax(b, n, g):
                dve.wait_ge(lg_ok, nth(lg_ok, b, n + 1))
                if n > 0:
                    dve.wait_ge(sub_ok, nth(sub_ok, b, n))
                dve.tensor_reduce(mx, lg_ps[g], AX.X, ALU.max).then_inc(max_ok, 1)
                dve.wait_ge(max_ok, nth(max_ok, b, n + 1))
                dve.tensor_tensor(logit[g % 2], lg_ps[g],
                                            mx.unsqueeze(2).to_broadcast([P, GRP, K]), ALU.subtract).then_inc(sub_ok, 1)

            def normalise(b, n, g):
                dve.wait_ge(exp_ok, nth(exp_ok, b, n + 1))
                if n > 0:
                    dve.wait_ge(att_ok, nth(att_ok, b, n))
                dve.tensor_reduce(sm, logit[g % 2], AX.X, ALU.add).then_inc(sm_ok, 1)
                dve.wait_ge(sm_ok, nth(sm_ok, b, n + 1))
                dve.reciprocal(ri, sm).then_inc(ri_ok, 1)
                dve.wait_ge(ri_ok, nth(ri_ok, b, n + 1))
                if n >= 2:
                    dve.wait_ge(alo_ok, nth(alo_ok, b, n - 1))
                    dve.wait_ge(asum_ok, nth(asum_ok, b, n - 1))
                dve.scalar_tensor_tensor(attn[g % 2], logit[g % 2], ATTN_SCALE,
                                                   ri.unsqueeze(2).to_broadcast([P, GRP, K]), ALU.mult, ALU.mult).then_inc(att_ok, 1)
                dve.wait_ge(att_ok, nth(att_ok, b, n + 1))
                dve.tensor_reduce(asum[:, g, :], attn[g % 2].rearrange("p i k -> p k i"), AX.X,
                                  ALU.add).then_inc(asum_ok, 1)

            def rebase(b, s):
                dve.wait_ge(ssum_ok, nth(ssum_ok, b, s + 1))
                dve.tensor_scalar(den, sum_ps, EPS_NORM * ATTN_SCALE, EPS_NORM, ALU.add, ALU.mult).then_inc(den_ok, 1)
                dve.wait_ge(den_ok, nth(den_ok, b, 3 * s + 1))
                dve.wait_ge(rt_ok, nth(rt_ok, b, s + 1))
                dve.tensor_tensor(den, den, rt, ALU.add).then_inc(den_ok, 1)
                dve.wait_ge(den_ok, nth(den_ok, b, 3 * s + 2))
                dve.reciprocal(den, den).then_inc(den_ok, 1)
                dve.wait_ge(den_ok, nth(den_ok, b, 3 * s + 3))
                dve.tensor_scalar(base, up_ps, den, BASE_SCALE, ALU.mult, ALU.mult).then_inc(base_ok, 1)
                if s < STAGES - 1:
                    dve.wait_ge(bhi_ok, nth(bhi_ok, b, s + 1))
                    dve.tensor_tensor(b_hl[:, :, 1, :], up_t, b_hl[:, :, 0, :], ALU.subtract).then_inc(blo_ok, 1)
                else:
                    dve.wait_ge(bhi_ok, nth(bhi_ok, b, s + 1))
                    dve.tensor_tensor(bT[:, 1, :], base, bT[:, 0, :], ALU.subtract).then_inc(blo_ok, 1)

            def add_x(b, t, j):
                if j % 2 == 0:
                    dve.wait_ge(xr_in[j // 2], nth(xr_in[j // 2], b, t + 1))
                dve.wait_ge(rec_ok, nth(rec_ok, b, t * NC + j + 1))
                dve.scalar_tensor_tensor(
                    feat[:, t, j * MM:(j + 1) * MM], mm_ps[j % 2] if t < 2 else rc_ps,
                    1.0 / (BASE_SCALE * ATTN_SCALE), stage[:, j * MM:(j + 1) * MM], ALU.mult, ALU.add,
                    accum_out=sums[t][:, j:j + 1]).then_inc(x1_ok, 1)

            def sum_c(b, t):
                dve.wait_ge(x1_ok, nth(x1_ok, b, (t + 1) * NC))
                dve.tensor_reduce(sm1[t], sums[t], AX.X, ALU.add).then_inc(c_sum, 1)

            def mean_c(b, t):
                dve.wait_ge(c_gm, nth(c_gm, b, t + 1))
                dve.tensor_scalar(nmg[t], st_ps[:, 0:1], -INV_N, None, ALU.mult).then_inc(c_nmg, 1)

            def var_c_(b, t):
                dve.wait_ge(c_gv, nth(c_gv, b, t + 1))
                dve.tensor_scalar(var_c[t], sd_ps, INV_N, EPS_GN, ALU.mult, ALU.add).then_inc(c_var, 1)

            def bias_c(b, t):
                dve.wait_ge(c_pow, nth(c_pow, b, t + 1))
                dve.tensor_tensor(nb_c[t], nmg[t], s_c[t], ALU.mult).then_inc(c_nb, 1)

            def depthwise(b, n):
                t, j = n // NR, n % NR
                dve.wait_ge(dwp_ok, nth(dwp_ok, b, n + 1))
                for i, k in enumerate(range(PE_TAPS, 9)):
                    dy, dx = k // 3, k % 3
                    if i > 0:
                        dve.wait_ge(tap_ok, nth(tap_ok, b, n * DVE_TAPS + i))
                    dve.scalar_tensor_tensor(
                        dw_ps[n % 3], img[:, j * ROWS + dy:(j + 1) * ROWS + dy, dx:dx + WW],
                        taps[:, t, k:k + 1], dw_ps[n % 3], ALU.mult, ALU.add).then_inc(tap_ok, 1)
                    c = 2 * NC + NC // 2 + 2 * n + i // 2
                    if i in (1, 3) and c - i // 2 + 1 < T * NC:
                        add_x(b, c // NC, c % NC)
                    if i == 2 and n % NR == 2 and n < NC:
                        mean_c(b, 2 + n // NR)
                    if i == 2 and n % NR == 0 and n < 3 * NR:
                        var_c_(b, 1 + n // NR)
                if n % NR == 1 and n < NC:
                    sum_c(b, 2 + n // NR)
                if n % NR == 0 and n < 3 * NR:
                    bias_c(b, 1 + n // NR)

            def prune(b, t):
                dve.wait_ge(hov_ok, nth(hov_ok, b, (t + 1) * NR))
                dve.tensor_reduce(hm1, hov[t % 2], AX.X, ALU.add).then_inc(hmax_ok, 1)
                dve.wait_ge(hmax_ok, nth(hmax_ok, b, t + 1))
                dve.tensor_scalar(mask1[:, t:t + 1], hm1, 0.0, None, ALU.is_gt).then_inc(mask1_ok, 1)
                dve.wait_ge(mask1_ok, nth(mask1_ok, b, t + 1))
                if t == 0:
                    dve.wait_ge(wl_in, nth(wl_in, b, 1))
                dve.tensor_scalar(w16[:, t], w16[:, t], mask1[:, t:t + 1], None, ALU.mult).then_inc(w_ok, 1)

            def finish(b, u):
                dve.wait_ge(rov_ok, nth(rov_ok, b, (u + 1) * NC))
                dve.tensor_reduce(rm1, rov[u % 2], AX.X, ALU.add).then_inc(rmax_ok, 1)
                dve.wait_ge(rmax_ok, nth(rmax_ok, b, u + 1))
                dve.tensor_scalar(mask2, rm1, 0.0, None, ALU.is_gt).then_inc(mask2_ok, 1)
                dve.wait_ge(mask2_ok, nth(mask2_ok, b, u + 1))
                dve.scalar_tensor_tensor(res[u % 2], res[u % 2], mask2, feat[:, u, :], ALU.mult, ALU.add).then_inc(y_ok, 1)

            def body(b, last):
                mine = [e for e in range(EARLY, NT) if EV_OWNER[e] == 'v']
                spread_a(b, T - 1)
                scale_a(b, T - 1)
                take_block(b, mine[0])
                take_block(b, mine[1])
                low_a(b, T - 1)
                for s in range(STAGES):
                    for g in range(NG + 1):
                        if s == 0 and g == 1:
                            for e in mine[2:]:
                                take_block(b, e)
                        if g < NG:
                            softmax(b, s * NG + g, g)
                        if g >= 1:
                            normalise(b, s * NG + g - 1, g - 1)
                    rebase(b, s)
                for j in range(NC):
                    add_x(b, 0, j)
                sum_c(b, 0)
                mean_c(b, 0)
                for j in range(NC):
                    add_x(b, 1, j)
                sum_c(b, 1)
                var_c_(b, 0)
                bias_c(b, 0)
                mean_c(b, 1)
                for j in range(NC // 2):
                    add_x(b, 2, j)
                for n in range(T * NR):
                    depthwise(b, n)
                    if n % NR == 2 and n > NR:
                        prune(b, n // NR - 1)
                prune(b, T - 1)
                if not last:
                    stats_a(b + 1, 0)
                    spread_a(b + 1, 0)
                    scale_a(b + 1, 0)
                finish(b, 0)
                if not last:
                    low_a(b + 1, 0)
                finish(b, 1)
                if not last:
                    stats_a(b + 1, 1)
                    spread_a(b + 1, 1)
                    scale_a(b + 1, 1)
                    low_a(b + 1, 1)
                finish(b, 2)
                if not last:
                    for e in (0, 2, 4):
                        take_block(b + 1, e)
                    stats_a(b + 1, 2)
                    spread_a(b + 1, 2)
                    scale_a(b + 1, 2)
                    low_a(b + 1, 2)
                    stats_a(b + 1, 3)
                finish(b, 3)

            n = [0]

            def step(ins):
                n[0] += 1
                ins.then_inc(setup_v, 1)
                dve.wait_ge(setup_v, n[0])

            dve.wait_ge(setup_t, 1)
            step(dve.tensor_copy(prm[:], banks[:, 7, 0:10 * T].rearrange("p (i t) -> p i t", t=T)))
            step(dve.tensor_scalar(prm[:, V1, :], prm[:, V1, :], EPS_BN, None, ALU.add))
            step(dve.tensor_scalar(prm[:, V2, :], prm[:, V2, :], EPS_BN, None, ALU.add))
            dve.wait_ge(setup_p, 3)
            step(dve.tensor_tensor(prm[:, G1, :], prm[:, G1, :], prm[:, V1, :], ALU.mult))
            step(dve.tensor_tensor(prm[:, G2, :], prm[:, G2, :], prm[:, V2, :], ALU.mult))
            step(dve.tensor_tensor(prm[:, DWB:DWB + 1, :], prm[:, DWB:DWB + 1, :], prm[:, M1:M1 + 1, :], ALU.subtract))
            step(dve.tensor_tensor(prm[:, PWB, :], prm[:, PWB, :], prm[:, M2, :], ALU.subtract))
            step(dve.tensor_tensor(prm[:, DWB, :], prm[:, DWB, :], prm[:, G1, :], ALU.mult))
            step(dve.tensor_tensor(prm[:, PWB, :], prm[:, PWB, :], prm[:, G2, :], ALU.mult))
            dve.wait_ge(bas_in, 16)
            step(dve.tensor_tensor(work[:, 2, 0:T * K], work[:, 0, 0:T * K], work[:, 0, 0:T * K], ALU.mult))
            dve.wait_ge(setup_t, 2)
            step(dve.tensor_copy(work[:, 1, 0:K], up_ps[:, 0:K]))
            dve.wait_ge(setup_p, 4)
            step(dve.tensor_scalar(work[:, 1, 0:K], work[:, 1, 0:K], EPS_NORM, None, ALU.add))
            step(dve.reciprocal(work[:, 1, 0:K], work[:, 1, 0:K]))
            for t in range(T):
                step(dve.scalar_tensor_tensor(work[:, 0, t * K:(t + 1) * K], work[:, 0, t * K:(t + 1) * K],
                                              BASE_SCALE, work[:, 1, 0:K], ALU.mult, ALU.mult))
                step(dve.tensor_copy(b0_hl[:, t, 0, :], work[:, 0, t * K:(t + 1) * K]))
                dve.tensor_tensor(b0_hl[:, t, 1, :], work[:, 0, t * K:(t + 1) * K], b0_hl[:, t, 0, :], ALU.subtract)
                dve.wait_ge(setup_a, t + 1)
                step(dve.tensor_tensor(w16[:, t, 1, :], banks[:, t, :], w16[:, t, 0, :], ALU.subtract))
                step(dve.tensor_scalar(taps[:, t, :], taps[:, t, :], prm[:, G1, t:t + 1], None, ALU.mult))
            assert n[0] == SETUP_V, n[0]
            dve.tensor_tensor(c1[:], prm[:, DWB, :], prm[:, B1, :], ALU.add)
            dve.tensor_tensor(c2[:], prm[:, PWB, :], prm[:, B2, :], ALU.add)
            dve.tensor_scalar(i2[:], prm[:, G2, :], 1.0 / PW_SCALE, None, ALU.mult).then_inc(setup_v, 1)
            for t in range(T - 1):
                stats_a(0, t)
                spread_a(0, t)
                scale_a(0, t)
                low_a(0, t)
            for e in (0, 2, 4):
                take_block(0, e)
            stats_a(0, T - 1)
            with dve.Fori(0, B - 1) as b:
                body(b, False)
            body(B - 1, True)

        @block.tensor
        def _(pe):
            mm = nc.tensor.matmul

            def stat_a(batch, t):
                pe.wait_ge(a_stat, nth(a_stat, batch, t + 1))
                mm(st_ps, gavg[:], mv, start=True, stop=True).then_inc(a_gm, 1)

            def spread_a(batch, t):
                pe.wait_ge(a_dev, nth(a_dev, batch, t + 1))
                mm(sd_ps, gavg[:], dev, start=True, stop=True).then_inc(a_gv, 1)

            def logits(bh, g, tiles):
                for i in range(GRP):
                    nt = g * GRP + i
                    px = slice(nt * P, (nt + 1) * P)
                    for t in tiles:
                        for fs, bs in ((0, 0), (0, 1), (1, 0)):
                            ins = mm(lg_ps[g][:, i, :], feat16[:, t, fs, px], bh[:, t, bs, :],
                                     start=(i == 0 and t == 0 and fs + bs == 0),
                                     stop=(t == T - 1 and fs == 1), skip_group_check=True)
                return ins

            def turn_block(b, e):
                if e >= 3:
                    own, ev = (evv_ok, EV_NTH[e - 3]) if EV_OWNER[e - 3] == 'v' else (eva_ok, EV_NTH[e - 3])
                    pe.wait_ge(own, nth(own, b, ev))
                pe.sem_inc(gate, 1)
                t, blk = BLOCKS[e]
                out_v = tr_ps[e % 3].rearrange("p (i s c) -> p i s c", s=2, c=P)
                for i in range(4):
                    for fs in range(2):
                        px = slice((4 * blk + i) * P, (4 * blk + i + 1) * P)
                        ins = nc.tensor.transpose(out_v[:, i, fs, :], feat16[:, t, fs, px], ident16[:])
                ins.then_inc(trx_ok, 1)

            def turn_attn(b, g):
                pe.wait_ge(alo_ok, nth(alo_ok, b, (STAGES - 1) * NG + g + 1))
                if g >= 2:
                    pe.wait_ge(aT_ok, nth(aT_ok, b, g - 1))
                pe.sem_inc(gate, 1)
                for i in range(GRP):
                    ins = nc.tensor.transpose(tr_ps[g % 2][:, i * P:(i + 1) * P],
                                              a_hl[:, g * GRP + i].rearrange("p s k -> p (s k)"), ident16[:])
                ins.then_inc(tra_ok, 1)

            def update(b, s, g):
                for i in range(GRP):
                    nt = g * GRP + i
                    first, end = nt == 0, nt == NT - 1
                    mm(up_ps, a_hl[:, nt].rearrange("p s k -> p (s k)"), featT[:, nt, 0, :],
                       start=first, stop=False, skip_group_check=True)
                    ins = mm(up_ps[0:K], a_hl[:, nt, 0, :], featT[:, nt, 1, :],
                             start=False, stop=end, skip_group_check=True)
                return ins

            def recon(b, c):
                t, j = c // NC, c % NC
                o = mm_ps[j % 2] if t < 2 else rc_ps
                if t >= 2:
                    pe.wait_ge(x1_ok, nth(x1_ok, b, c))
                elif c >= 2:
                    pe.wait_ge(x1_ok, nth(x1_ok, b, c - 1))
                mm(o, bT[:, 0, t * P:(t + 1) * P], aT[:, 4 * j:4 * j + 4, :], start=True, stop=False)
                mm(o, bT[0:K, 1, t * P:(t + 1) * P], aT[0:K, 4 * j:4 * j + 4, :],
                   start=False, stop=True).then_inc(rec_ok, 1)

            def depthwise(b, n):
                t, j = n // NR, n % NR
                if j == 0:
                    pe.wait_ge(diag_ok, nth(diag_ok, b, t + 1))
                if n == 2:
                    pe.wait_ge(x1_ok, nth(x1_ok, b, 2 * NC))
                if n >= 3:
                    pe.wait_ge(h32_ok, nth(h32_ok, b, n - 2))
                for h in range(2):
                    c = 2 * NC + NC // 2 + 2 * (n - 1) + h
                    if n > 0 and c < T * NC:
                        recon(b, c)
                    pe.wait_ge(img_ok, nth(img_ok, b, t * NR + min(j + 1 + h, NR)))
                    o = banks[:, 2 * (n % 3) + h, :].rearrange("p (h w) -> p h w", w=WW)
                    for k in range(PE_TAPS):
                        r = j * ROWS + h * ROWS // 2 + k // 3
                        ins = mm(o, diag[:, t % 2, k, :], img[:, r:r + ROWS // 2, k % 3:k % 3 + WW],
                                 start=(k == 0), stop=(k == PE_TAPS - 1))
                        if n == 0 and k % 2 == 0:
                            recon(b, 2 * NC + 2 * h + k // 2)
                ins.then_inc(dwp_ok, 1)

            def pointwise(b, u, j):
                n = u * NC + j
                if n >= 4:
                    pe.wait_ge(r_ok, nth(r_ok, b, n - 3))
                else:
                    pe.wait_ge(h32_ok, nth(h32_ok, b, T * NR - 2 + n // 2 * 2))
                if u == 0:
                    pe.wait_ge(hlo_ok, nth(hlo_ok, b, (T - 1) * NR + j // 2 + 1))
                for t in range(T):
                    if n == 0:
                        pe.wait_ge(w_ok, nth(w_ok, b, t + 1))
                    for ws, hs in ((0, 0), (0, 1), (1, 0)):
                        ins = mm(pw_ps[n % 4], w16[:, t, ws, u * P:(u + 1) * P], hid[:, j, t, hs, :],
                                 start=(t == 0 and ws + hs == 0), stop=(t == T - 1 and ws == 1))
                ins.then_inc(pw_ok, 1)

            def body(b, last):
                for s in range(STAGES):
                    if s == 0:
                        for g in range(NG):
                            logits(b0_hl, g, [0])
                        stat_a(b, T - 1)
                        for g in range(NG):
                            logits(b0_hl, g, [1])
                        spread_a(b, T - 1)
                        pe.wait_ge(a_lov, nth(a_lov, b, T - 1))
                        pe.wait_ge(a_lop, nth(a_lop, b, T - 1))
                        for g in range(NG):
                            logits(b0_hl, g, [2])
                        for e in range(EARLY, EARLY + 5):
                            turn_block(b, e)
                        pe.wait_ge(a_lov, nth(a_lov, b, T))
                        pe.wait_ge(a_lop, nth(a_lop, b, T))
                        for g in range(NG):
                            logits(b0_hl, g, [T - 1]).then_inc(lg_ok, 1)
                        for e in range(EARLY + 5, NT):
                            turn_block(b, e)
                        pe.wait_ge(evv_ok, nth(evv_ok, b, EV_DVE))
                        pe.wait_ge(eva_ok, nth(eva_ok, b, NT - EV_DVE))
                    else:
                        pe.wait_ge(blo_ok, nth(blo_ok, b, s))
                        for g in range(NG):
                            logits(b_hl, g, range(T)).then_inc(lg_ok, 1)
                    for g in range(NG):
                        pe.wait_ge(alo_ok, nth(alo_ok, b, s * NG + g + 1))
                        ins = update(b, s, g)
                    ins.then_inc(up_ok, 1)
                    if s == STAGES - 1:
                        for g in range(NG):
                            turn_attn(b, g)
                    pe.wait_ge(asum_ok, nth(asum_ok, b, (s + 1) * NG))
                    for half in range(2):
                        for g in range(NG):
                            ins = mm(sum_ps[half * K:(half + 1) * K], asum[:, g, :], one_c,
                                     start=(g == 0), stop=(g == NG - 1))
                    ins.then_inc(ssum_ok, 1)
                    pe.wait_ge(upc_ok, nth(upc_ok, b, s + 1))
                    mm(up_ps, fold[:], upd, start=True, stop=True).then_inc(fold_ok, 1)
                    if s < STAGES - 1:
                        pe.wait_ge(base_ok, nth(base_ok, b, s + 1))
                        pe.wait_ge(n2_ok, nth(n2_ok, b, s + 1))
                        pe.sem_inc(gate, 1)
                        for t in range(T):
                            ins = nc.tensor.transpose(up_t[:, t, :], base[0:K, t * P:(t + 1) * P], ident[0:K, 0:K])
                        ins.then_inc(bt_ok, 1)
                pe.wait_ge(blo_ok, nth(blo_ok, b, STAGES))
                pe.wait_ge(aT_ok, nth(aT_ok, b, NG))

                def mean_c(t):
                    pe.wait_ge(c_sum, nth(c_sum, b, t + 1))
                    if t > 0:
                        pe.wait_ge(c_var, nth(c_var, b, t))
                    mm(st_ps[:, 0:1], gavg[:], sm1[t], start=True, stop=True).then_inc(c_gm, 1)

                def var_c_(t):
                    pe.wait_ge(c_sq, nth(c_sq, b, t + 1))
                    mm(sd_ps, gavg[:], sq[t], start=True, stop=True).then_inc(c_gv, 1)

                for c in range(NC):
                    recon(b, c)
                mean_c(0)
                for c in range(NC, 2 * NC):
                    recon(b, c)
                var_c_(0)
                mean_c(1)
                for n in range(T * NR):
                    if n % NR == 1 and n < 3 * NR:
                        var_c_(1 + n // NR)
                    if n % NR == 3 and n < NC:
                        mean_c(2 + n // NR)
                    depthwise(b, n)
                for u in range(T):
                    for j in range(NC):
                        pointwise(b, u, j)
                        if last:
                            continue
                        if (u, j) == (0, 2):
                            stat_a(b + 1, 0)
                        if (u, j) == (0, 4):
                            spread_a(b + 1, 0)
                        if (u, j) == (2, 3):
                            stat_a(b + 1, 1)
                        if (u, j) == (2, 4):
                            spread_a(b + 1, 1)
                        if (u, j) == (3, 4):
                            stat_a(b + 1, 2)
                        if (u, j) == (3, 5):
                            spread_a(b + 1, 2)
                        if u == T - 1:
                            if j == 0:
                                pe.wait_ge(a_lov, nth(a_lov, b + 1, 2))
                                pe.wait_ge(a_lop, nth(a_lop, b + 1, 2))
                            turn_block(b + 1, 2 * j)
                            turn_block(b + 1, 2 * j + 1)
                if not last:
                    pe.wait_ge(r_ok, nth(r_ok, b, T * NC))

            pe.wait_ge(const_ok, 1)
            pe.wait_ge(prm_in, 16 * 11)
            nc.tensor.transpose(banks[:, 7, 0:10 * T], prm_rows, ident[0:10 * T, 0:10 * T]).then_inc(setup_t, 1)
            pe.wait_ge(setup_v, 10)
            for t in range(T):
                ins = mm(up_ps[:, 0:K], onesf, work[:, 2, t * K:(t + 1) * K], start=(t == 0), stop=(t == T - 1))
            ins.then_inc(setup_t, 1)
            pe.wait_ge(w_in, 16)
            for t in range(T):
                for u in range(T):
                    ins = mm(banks[:, t, u * P:(u + 1) * P], stage[:, u * C + t * P:u * C + (t + 1) * P], scaled,
                             start=True, stop=True)
                ins.then_inc(setup_t, 1)
            for t in range(T - 1):
                stat_a(0, t)
                spread_a(0, t)
            pe.wait_ge(a_lov, T - 1)
            pe.wait_ge(a_lop, T - 1)
            for e in range(EARLY):
                turn_block(0, e)
            with pe.Fori(0, B - 1) as b:
                body(b, False)
            body(B - 1, True)


_INS = ['x', 'L0_conv_bases', 'L1_conv_dw_w', 'L1_conv_dw_b', 'L1_conv_bn1_g', 'L1_conv_bn1_b', 'L1_conv_bn1_m',
        'L1_conv_bn1_v', 'L1_conv_pw_w', 'L1_conv_pw_b', 'L1_conv_bn2_g', 'L1_conv_bn2_b', 'L1_conv_bn2_m',
        'L1_conv_bn2_v']


def kernel(**inputs):
    import numpy as _np
    import concourse.bacc as _bacc
    from concourse import mybir as _mybir
    from concourse.bass_utils import run_bass_kernel_spmd as _run

    nc = _bacc.Bacc("TRN2", target_bir_lowering=False, num_devices=1)
    arrays, args = {}, []
    for name in _INS:
        a = _np.ascontiguousarray(inputs[name])
        arrays[f"in_{name}_dram"] = a
        args.append(nc.dram_tensor(f"in_{name}_dram", a.shape, _mybir.dt.from_np(a.dtype), kind="ExternalInput").ap())
    shape = inputs['x'].shape
    args.append(nc.dram_tensor("out_0_dram", shape, _mybir.dt.float32, kind="ExternalOutput").ap())
    conv_preact_block(nc, *args)
    r = _run(nc, [arrays], core_ids=[0])
    return r.results[0]["out_0_dram"]
```

```python
from contextlib import ExitStack

import numpy as np

import concourse.bass as bass
from concourse import mybir

F32 = mybir.dt.float32
F16 = mybir.dt.float16
ALU = mybir.AluOpType
ACT = mybir.ActivationFunctionType
AX = mybir.AxisListType

P = 128
GROUP = 16
STAGES = 3
EPS_NORM = 1e-6
EPS_GN = 1e-5
EPS_BN = 1e-5
DW_THRESH = 4.0
PW_THRESH = 0.001
BASE_SCALE = 2.0 ** 10
ATTN_SCALE = 2.0 ** 14
PW_SCALE = 2.0 ** 6
PE_TAPS = 4
ROWS = 16
MM = 512


def below(x):
    return float(np.nextafter(np.float32(x), np.float32(0.0)))


def conv_preact_block(
    nc, x, bases, dw_w, dw_b, bn1_g, bn1_b, bn1_m, bn1_v, pw_w, pw_b, bn2_g, bn2_b, bn2_m, bn2_v, out,
):
    B, C, HH, WW = x.shape
    K = bases.shape[2]
    N = HH * WW
    T = C // P
    NT = N // P
    GRP = MM // K
    NG = NT // GRP
    NC = N // MM
    NR = HH // ROWS
    CH = ROWS * WW
    LOP = N // 4
    PW = WW + 2
    DVE_TAPS = 9 - PE_TAPS
    INV_N = 1.0 / N
    BLOCKS = [(i % 2, i // 2) for i in range(NT // 2)] + [(t, i) for t in (2, 3) for i in range(NT // 4)]
    EARLY = NT // 2
    EV_VECTOR = (0, 1, 3, 5, 8, 9, 12, 13, 15, 16, 18, 20, 23, 25, 27, 29, 31)
    EV_OWNER = ['v' if e in EV_VECTOR else 'a' for e in range(NT)]
    EV_DVE = EV_OWNER.count('v')
    EV_NTH = [EV_OWNER[:e + 1].count(EV_OWNER[e]) for e in range(NT)]
    assert C == 512 and K == 64 and CH == 2 * MM and T == 4

    xv = x.rearrange("b (t p) h w -> b t p (h w)", p=P)
    ov = out.rearrange("b (t p) h w -> b t p (h w)", p=P)
    w_dram = nc.dram_tensor("pw_split", [P, T * 2 * C], F16, kind="Internal").ap()

    with ExitStack() as ctx:
        def sb(name, shape, dt):
            return ctx.enter_context(nc.sbuf_tensor(name, shape, dt))

        step_of = {}

        def sem(name, per, unit=1):
            s = ctx.enter_context(nc.semaphore(name))
            step_of[s] = (per, unit)
            return s

        def nth(s, batch, k):
            per, unit = step_of[s]
            return batch * (per * unit) + k * unit

        feat = sb("feat", [P, T, N], F32)
        feat16 = feat[:].rearrange("p t n -> p (t n)").bitcast(F16).rearrange("p (t s n) -> p t s n", t=T, s=2)
        pix = sb("pix", [P, NT * 2 * C], F16)
        featT = pix[:].rearrange("p (i s c) -> p i s c", s=2, c=C)
        hid = pix[:].rearrange("p (j t s m) -> p j t s m", t=T, s=2, m=MM)
        stage = sb("stage", [P, N], F32)
        pad = sb("pad", [P, (HH + 2) * PW], F32)
        img = pad[:].rearrange("p (h w) -> p h w", w=PW)
        att = sb("att", [P, N], F32)
        att16 = att[:].bitcast(F16)
        a_hl = att16[:, 0:N].rearrange("p (i s k) -> p i s k", s=2, k=K)
        aT = att16[:, N:2 * N].rearrange("p (i n) -> p i n", n=P)
        pix32 = pix[:].bitcast(F32).rearrange("p (j t m) -> p j t m", t=T, m=MM)
        stage16 = stage[:].bitcast(F16).rearrange("p (s n) -> p s n", s=2)
        halves = [feat16[:, t] for t in range(T - 1)] + [stage16]
        x_st = [stage[:], pad[:, 0:N], stage[:], pad[:, 0:N]]
        res = att
        w16 = sb("w16", [P, T, 2, C], F16)
        diag = sb("diag", [P, 2, PE_TAPS, P], F32)
        upd = diag[:].rearrange("p a b c -> p (a b c)")[:, 0:C]
        base = diag[:].rearrange("p a b c -> p (a b c)")[:, C:2 * C]
        work = sb("work", [P, 4, MM], F32)
        logit = [work[:, i, :].rearrange("p (i k) -> p i k", k=K) for i in range(2)]
        attn = [work[:, 2 + i, :].rearrange("p (i k) -> p i k", k=K) for i in range(2)]
        h32 = [work[:, 2 * i:2 * i + 2, :] for i in range(2)]
        bT = sb("bT", [P, 2, C], F16)
        b_hl = sb("b_hl", [P, T, 2, K], F16)
        b0_hl = sb("b0_hl", [P, T, 2, K], F16)
        ident = sb("ident", [P, P], F32)
        ident16 = sb("ident16", [P, P], F16)
        fold = sb("fold", [P, P], F32)
        gavg = sb("gavg", [P, P], F32)
        onesf, scaled, prm_rows = pad[:, 0:P], pad[:, P:2 * P], pad[0:10 * T, 2 * P:3 * P]
        asum = sb("asum", [P, NG, K], F32)
        small = sb("small", [P, 180], F32)
        col = lambda i, n=1: small[:, i:i + n]
        half_c, mhalf_c, one_c, dwt_c, pwt_c = col(0), col(1), col(10), col(11), col(36)
        bn_s = sb("bn_s", [P, NC, 6], F32)
        mv, dev, gm, var_a, s_a, nb_a = col(2, 2), col(4), col(5, 2), col(7), col(8), col(9)
        mx, sm, ri = col(12, GRP), col(20, GRP), col(28, GRP)
        n2, rt, den = col(37), col(38), col(39)
        sums, sm1, nmg, sq, var_c, s_c, nb_c = (
            [col(o + i * w, w) for i in range(T)]
            for o, w in ((80, NC), (140, 1), (144, 1), (148, 1), (152, 1), (156, 1), (160, 1)))
        hov = [col(40 + i * NR, NR) for i in range(2)]
        rov = [col(124 + i * NC, NC) for i in range(2)]
        hm1 = col(58)
        mask1 = col(60, T)
        rm1, mask2 = col(68), col(69)
        prm = sb("prm", [P, 10, T], F32)
        DWB, G1, B1, M1, V1, PWB, G2, B2, M2, V2 = range(10)
        taps = sb("taps", [P, T, 9], F32)
        c1 = sb("c1", [P, T], F32)
        i2 = sb("i2", [P, T], F32)
        c2 = sb("c2", [P, T], F32)

        banks = ctx.enter_context(nc.psum_tensor("banks", [P, 8, MM], F32))
        lg_ps = [banks[:, g, :].rearrange("p (i k) -> p i k", k=K) for g in range(4)]
        dw_ps = [banks[:, 2 * i:2 * i + 2, :].rearrange("p a (h w) -> p (a h) w", w=WW) for i in range(3)]
        mm_ps = [banks[:, i, :] for i in range(6)]
        up_ps = banks[:, 6, :]
        rc_ps = banks[:, 6, :]
        up_t = banks[:, 6, 0:T * K].rearrange("p (t k) -> p t k", k=K)
        tr_ps = [banks[:, 4 + i, :].bitcast(F16) for i in range(3)]
        pw_ps = [banks[:, i, :] for i in (2, 3, 4, 5)] + [banks[:, (2, 3, 0, 1)[n % 4], :] for n in range(4, T * NC)]
        sum_ps = banks[:, 7, 0:1]
        st_ps = banks[:, 7, 0:2]
        sd_ps = banks[:, 7, 2:3]

        prm_in = sem("prm_in", 1, 16)
        w_in = sem("w_in", 1, 16)
        bas_in = sem("bas_in", 1, 16)
        const_ok = sem("const_ok", 1)
        setup_p = sem("setup_p", 1)
        setup_v = sem("setup_v", 1)
        setup_a = sem("setup_a", 1)
        setup_t = sem("setup_t", 1)
        w_saved = sem("w_saved", 1, 16)
        gate = ctx.enter_context(nc.semaphore("gate"))
        x_in = [sem(f"x_in{t}", 1, 16) for t in range(T)]
        a_stat = sem("a_stat", T)
        a_gm = sem("a_gm", T)
        a_dev = sem("a_dev", T)
        a_gv = sem("a_gv", T)
        a_var = sem("a_var", T)
        a_pow = sem("a_pow", T)
        a_nb = sem("a_nb", T)
        a_norm = sem("a_norm", T)
        a_hi = sem("a_hi", 2 * T)
        a_lov = sem("a_lov", T)
        a_lop = sem("a_lop", T)
        bns_ok = sem("bns_ok", T)
        gmc_ok = sem("gmc_ok", T)
        dif_ok = sem("dif_ok", T)
        trx_ok = sem("trx_ok", NT)
        evv_ok = sem("evv_ok", EV_DVE)
        eva_ok = sem("eva_ok", NT - EV_DVE)
        lg_ok = sem("lg_ok", STAGES * NG)
        sub_ok = sem("sub_ok", STAGES * NG)
        exp_ok = sem("exp_ok", STAGES * NG)
        att_ok = sem("att_ok", STAGES * NG)
        ahi_ok = sem("ahi_ok", STAGES * NG)
        alo_ok = sem("alo_ok", STAGES * NG)
        max_ok = sem("max_ok", STAGES * NG)
        sm_ok = sem("sm_ok", STAGES * NG)
        ri_ok = sem("ri_ok", STAGES * NG)
        den_ok = sem("den_ok", STAGES * 3)
        asum_ok = sem("asum_ok", STAGES * NG)
        ssum_ok = sem("ssum_ok", STAGES)
        up_ok = sem("up_ok", STAGES)
        upc_ok = sem("upc_ok", STAGES)
        fold_ok = sem("fold_ok", STAGES)
        n2_ok = sem("n2_ok", STAGES)
        rt_ok = sem("rt_ok", STAGES)
        base_ok = sem("base_ok", STAGES)
        bt_ok = sem("bt_ok", STAGES - 1)
        bhi_ok = sem("bhi_ok", STAGES)
        blo_ok = sem("blo_ok", STAGES)
        tra_ok = sem("tra_ok", NG)
        aTv_ok = sem("aTv_ok", NG - 2)
        aTa_ok = sem("aTa_ok", 2)
        xr_in = [sem(f"xr_in{i}", T, 16) for i in range(NR)]
        rec_ok = sem("rec_ok", T * NC)
        x1_ok = sem("x1_ok", T * NC)
        c_sum = sem("c_sum", T)
        c_gm = sem("c_gm", T)
        c_nmg = sem("c_nmg", T)
        c_sq = sem("c_sq", T)
        c_gv = sem("c_gv", T)
        c_var = sem("c_var", T)
        c_pow = sem("c_pow", T)
        c_nb = sem("c_nb", T)
        brd_ok = sem("brd_ok", 1)
        wl_in = sem("wl_in", 1, 16)
        diag_ok = sem("diag_ok", T)
        img_ok = sem("img_ok", T * NR)
        dwp_ok = sem("dwp_ok", T * NR)
        tap_ok = sem("tap_ok", T * NR * DVE_TAPS)
        hov_ok = sem("hov_ok", T * NR)
        h32_ok = sem("h32_ok", T * NR)
        hhi_ok = sem("hhi_ok", T * NR)
        hlo_ok = sem("hlo_ok", T * NR)
        hmax_ok = sem("hmax_ok", T)
        mask1_ok = sem("mask1_ok", T)
        w_ok = sem("w_ok", T)
        pw_ok = sem("pw_ok", T * NC)
        r_ok = sem("r_ok", T * NC)
        rov_ok = sem("rov_ok", T * NC)
        rmax_ok = sem("rmax_ok", T)
        mask2_ok = sem("mask2_ok", T)
        y_ok = sem("y_ok", 2 * T)
        y_out = [sem(f"y_out{u}", 1, 16) for u in range(T)]

        SETUP_V = 13 + 4 * T

        def place_T(e):
            t, i = BLOCKS[e]
            return featT[:, 4 * i:4 * i + 4, :, t * P:(t + 1) * P]

        block = ctx.enter_context(nc.Block())

        @block.sync
        def _(sp):
            def load_x(batch, t):
                if t >= 2:
                    sp.wait_ge(a_lov, nth(a_lov, batch, t - 1))
                    sp.wait_ge(a_lop, nth(a_lop, batch, t - 1))
                sp.dma_start(x_st[t], xv[bass.ds(batch, 1), t].rearrange("a p n -> (a p) n")).then_inc(
                    x_in[t], 16)

            def body(b, last):
                for t in range(T):
                    for j in range(NR):
                        if t > 0:
                            sp.wait_ge(x1_ok, nth(x1_ok, b, (t - 1) * NC + 2 * j + 2))
                        elif j == 0:
                            sp.wait_ge(lg_ok, nth(lg_ok, b, STAGES * NG))
                        sp.dma_start(stage[:, j * CH:(j + 1) * CH],
                                     xv[bass.ds(b, 1), t, :, j * CH:(j + 1) * CH].rearrange("a p n -> (a p) n")
                                     ).then_inc(xr_in[j], 16)
                    if t == 0:
                        sp.dma_start(w16[:].rearrange("p t s c -> p (t s c)"), w_dram).then_inc(wl_in, 16)
                if not last:
                    sp.wait_ge(x1_ok, nth(x1_ok, b, T * NC))
                    load_x(b + 1, 0)
                    sp.wait_ge(tap_ok, nth(tap_ok, b, T * NR * DVE_TAPS))
                    load_x(b + 1, 1)
                for u in range(T):
                    sp.wait_ge(y_ok, nth(y_ok, b, 2 * u + 2))
                    sp.dma_start(ov[bass.ds(b, 1), u].rearrange("a p n -> (a p) n"),
                                 feat[:, u, :]).then_inc(y_out[u], 16)
                    if not last and u < 2:
                        load_x(b + 1, u + 2)

            for i, a in enumerate((dw_b, bn1_g, bn1_b, bn1_m, bn1_v, pw_b, bn2_g, bn2_b, bn2_m, bn2_v)):
                sp.dma_start(prm_rows[i * T:(i + 1) * T, :], a.rearrange("(t p) -> t p", p=P)).then_inc(prm_in, 16)
            sp.dma_start(taps[:], dw_w.rearrange("(t p) o h w -> p t (o h w)", p=P)).then_inc(prm_in, 16)
            sp.dma_start(stage[:, 0:T * C].rearrange("p (u c) -> p u c", u=T),
                         pw_w.rearrange("(u p) c h w -> p u (c h w)", p=P)).then_inc(w_in, 16)
            sp.dma_start(work[:, 0, 0:T * K].rearrange("p (t k) -> p t k", t=T),
                         bases.rearrange("o (t p) k -> p t (o k)", p=P)).then_inc(bas_in, 16)
            sp.wait_ge(setup_v, SETUP_V)
            sp.dma_start(w_dram, w16[:].rearrange("p t s c -> p (t s c)")).then_inc(w_saved, 16)
            sp.wait_ge(setup_t, 2 + T)
            for t in range(T):
                load_x(0, t)
            with sp.Fori(0, B - 1) as b:
                body(b, False)
            body(B - 1, True)
            for u in range(T):
                sp.wait_ge(y_out[u], nth(y_out[u], B, 0))

        @block.gpsimd
        def _(pool):
            def lo_a(batch, t):
                pool.wait_ge(a_hi, nth(a_hi, batch, 2 * t + 2))
                pool.tensor_tensor(halves[t][:, 1, 0:LOP], x_st[t][:, 0:LOP],
                                   halves[t][:, 0, 0:LOP], ALU.subtract).then_inc(a_lop, 1)

            def pow_a(batch, t):
                pool.wait_ge(a_var, nth(a_var, batch, t + 1))
                pool.tensor_tensor(s_a, var_a, mhalf_c, ALU.pow).then_inc(a_pow, 1)

            def body(b, last):
                for s in range(STAGES):
                    for g in range(NG):
                        n = s * NG + g
                        pool.wait_ge(ahi_ok, nth(ahi_ok, b, n + 1))
                        pool.tensor_tensor(a_hl[:, g * GRP:(g + 1) * GRP, 1, :], attn[g % 2],
                                           a_hl[:, g * GRP:(g + 1) * GRP, 0, :],
                                           ALU.subtract).then_inc(alo_ok, 1)
                    pool.wait_ge(n2_ok, nth(n2_ok, b, s + 1))
                    pool.tensor_tensor(rt, n2, half_c, ALU.pow).then_inc(rt_ok, 1)
                pool.wait_ge(a_lov, nth(a_lov, b, T))
                pool.sem_inc(gate, 1)
                pool.memset(pad[:], 0.0).then_inc(brd_ok, 1)

                def pow_c(t):
                    pool.wait_ge(c_var, nth(c_var, b, t + 1))
                    pool.tensor_tensor(s_c[t], var_c[t], mhalf_c, ALU.pow).then_inc(c_pow, 1)

                pow_c(0)
                pow_c(1)
                for t in range(T):
                    for j in range(NR):
                        n = t * NR + j
                        if j == 3 and t + 2 < T:
                            pow_c(t + 2)
                        pool.wait_ge(hhi_ok, nth(hhi_ok, b, n + 1))
                        pool.tensor_tensor(hid[:, 2 * j:2 * j + 2, t, 1, :], h32[n % 2],
                                           hid[:, 2 * j:2 * j + 2, t, 0, :], ALU.subtract).then_inc(hlo_ok, 1)
                if not last:
                    pow_a(b + 1, 0)
                    for t in range(1, T):
                        pow_a(b + 1, t)
                        lo_a(b + 1, t - 1)
                    lo_a(b + 1, T - 1)

            pool.memset(ident[:], 0.0)
            pool.memset(ident16[:], 0.0)
            pool.memset(fold[:], 0.0)
            pool.memset(gavg[:], 1.0 / GROUP)
            pool.memset(one_c, 1.0)
            pool.memset(dwt_c, -below(DW_THRESH))
            pool.memset(pwt_c, -below(PW_THRESH))
            pool.memset(onesf, 1.0)
            pool.memset(scaled, 0.0)
            pool.memset(half_c, 0.5)
            pool.memset(mhalf_c, -0.5).then_inc(setup_p, 1)
            pool.wait_ge(setup_p, 1)
            pool.affine_select(out=ident[:], in_=ident[:], compare_op=ALU.not_equal, fill=1.0, base=0,
                               pattern=[[-1, P]], channel_multiplier=1)
            pool.affine_select(out=scaled, in_=scaled, compare_op=ALU.not_equal, fill=PW_SCALE, base=0,
                               pattern=[[-1, P]], channel_multiplier=1)
            pool.affine_select(out=ident16[:], in_=ident16[:], compare_op=ALU.not_equal, fill=1.0, base=0,
                               pattern=[[-1, P]], channel_multiplier=1)
            fv = fold[:].rearrange("p (a k) -> p a k", a=2)
            pool.affine_select(out=fv, in_=fv, compare_op=ALU.not_equal, fill=1.0, base=0,
                               pattern=[[0, 2], [-1, K]], channel_multiplier=1)
            gv = gavg[:].rearrange("p (a k) -> p a k", k=GROUP)
            pool.affine_select(out=gv, in_=gv, compare_op=ALU.is_ge, fill=0.0, base=0,
                               pattern=[[-GROUP, P // GROUP], [0, GROUP]], channel_multiplier=1).then_inc(setup_p, 1)
            pool.wait_ge(setup_p, 2)
            pool.affine_select(out=fv, in_=fv, compare_op=ALU.not_equal, fill=1.0, base=-K,
                               pattern=[[0, 2], [-1, K]], channel_multiplier=1)
            pool.affine_select(out=gv, in_=gv, compare_op=ALU.is_ge, fill=0.0, base=GROUP - 1,
                               pattern=[[GROUP, P // GROUP], [0, GROUP]], channel_multiplier=-1).then_inc(const_ok, 1)
            pool.wait_ge(setup_v, 3)
            pool.tensor_tensor(prm[:, V1, :], prm[:, V1, :], mhalf_c.to_broadcast([P, T]), ALU.pow)
            pool.tensor_tensor(prm[:, V2, :], prm[:, V2, :], mhalf_c.to_broadcast([P, T]), ALU.pow).then_inc(setup_p, 1)
            pool.wait_ge(setup_v, 11)
            pool.tensor_tensor(work[:, 1, 0:K], work[:, 1, 0:K], half_c.to_broadcast([P, K]),
                               ALU.pow).then_inc(setup_p, 1)
            for t in range(T):
                pow_a(0, t)
                lo_a(0, t)
            with pool.Fori(0, B - 1) as b:
                body(b, False)
            body(B - 1, True)

        @block.scalar
        def _(act):
            def hi_a(batch, t, h, b_free):
                act.wait_ge(a_norm, nth(a_norm, batch, t + 1))
                if b_free is not None and t < T - 1:
                    act.wait_ge(y_out[t], nth(y_out[t], b_free, 1))
                if t == T - 1:
                    act.wait_ge(a_lov, nth(a_lov, batch, t))
                    act.wait_ge(a_lop, nth(a_lop, batch, t))
                px = slice(h * N // 2, (h + 1) * N // 2)
                act.activation(halves[t][:, 0, px], x_st[t][:, px], ACT.Identity).then_inc(a_hi, 1)

            def squares(b, t):
                act.wait_ge(c_nmg, nth(c_nmg, b, t + 1))
                act.activation(pix32[:, :, t, :], feat[:, t, :].rearrange("p (j m) -> p j m", m=MM),
                               ACT.Square, bias=nmg[t], accum_out=sq[t]).then_inc(c_sq, 1)

            def image(b, t, j):
                if j == 0:
                    act.wait_ge(c_nb, nth(c_nb, b, t + 1))
                    if t == 0:
                        act.wait_ge(brd_ok, nth(brd_ok, b, 1))
                if t > 0:
                    act.wait_ge(tap_ok, nth(tap_ok, b, ((t - 1) * NR + min(j + 2, NR)) * DVE_TAPS))
                act.activation(img[:, 1 + j * ROWS:1 + (j + 1) * ROWS, 1:1 + WW],
                               feat[:, t, j * CH:(j + 1) * CH].rearrange("p (h w) -> p h w", w=WW),
                               ACT.Identity, bias=nb_c[t], scale=s_c[t]).then_inc(img_ok, 1)

            def diagonals(b, t):
                if t > 1:
                    act.wait_ge(dwp_ok, nth(dwp_ok, b, (t - 1) * NR))
                for k in range(PE_TAPS):
                    ins = act.activation(diag[:, t % 2, k, :], ident[:], ACT.Identity, scale=taps[:, t, k:k + 1])
                ins.then_inc(diag_ok, 1)

            def hidden(b, t, j):
                n = t * NR + j
                if t + 1 < T and j > 0:
                    image(b, t + 1, j - 1)
                act.wait_ge(tap_ok, nth(tap_ok, b, (n + 1) * DVE_TAPS))
                if n >= 2:
                    act.wait_ge(hlo_ok, nth(hlo_ok, b, n - 1))
                hv = h32[n % 2].rearrange("p a (h w) -> p (a h) w", w=WW)
                act.activation(hv, dw_ps[n % 3], ACT.Relu, bias=c1[:, t:t + 1]).then_inc(h32_ok, 1)
                if t + 1 < T and j == NR - 1:
                    image(b, t + 1, j)
                act.wait_ge(h32_ok, nth(h32_ok, b, n + 1))
                if t >= 2 and j == 0:
                    act.wait_ge(hmax_ok, nth(hmax_ok, b, t - 1))
                act.activation(hid[:, 2 * j:2 * j + 2, t, 1, :], h32[n % 2], ACT.Relu, bias=dwt_c,
                               accum_out=hov[t % 2][:, j:j + 1]).then_inc(hov_ok, 1)
                act.activation(hid[:, 2 * j:2 * j + 2, t, 0, :], h32[n % 2], ACT.Identity).then_inc(hhi_ok, 1)

            def result(b, u, j):
                n = u * NC + j
                act.wait_ge(pw_ok, nth(pw_ok, b, n + 1))
                if u > 0 and j % (NC // 2) == 0:
                    act.wait_ge(y_ok, nth(y_ok, b, 2 * u - 1 + j // (NC // 2)))
                act.activation(res[:, j * MM:(j + 1) * MM], pw_ps[n], ACT.Relu,
                               bias=c2[:, u:u + 1], scale=i2[:, u:u + 1]).then_inc(r_ok, 1)

            def over(b, u, j):
                n = u * NC + j
                act.wait_ge(r_ok, nth(r_ok, b, n + 1))
                if n >= 4:
                    act.wait_ge(rov_ok, nth(rov_ok, b, n - 3))
                else:
                    act.wait_ge(hlo_ok, nth(hlo_ok, b, T * NR - 1 + n // 2))
                if u >= 2 and j == 0:
                    act.wait_ge(rmax_ok, nth(rmax_ok, b, u - 1))
                act.activation(work[:, n % 4, :], res[:, j * MM:(j + 1) * MM], ACT.Relu, bias=pwt_c,
                               accum_out=rov[u % 2][:, j:j + 1]).then_inc(rov_ok, 1)

            def take_block(b, e):
                act.wait_ge(trx_ok, nth(trx_ok, b, e + 1))
                act.activation(place_T(e),
                               tr_ps[e % 3].rearrange("p (i s c) -> p i s c", s=2, c=P),
                               ACT.Identity).then_inc(eva_ok, 1)

            def body(b, last):
                def exponentials(s, g):
                    n = s * NG + g
                    act.wait_ge(sub_ok, nth(sub_ok, b, n + 1))
                    act.activation(logit[g % 2], logit[g % 2], ACT.Exp, scale=1.0 / BASE_SCALE).then_inc(exp_ok, 1)

                def high(s, g):
                    n = s * NG + g
                    act.wait_ge(att_ok, nth(att_ok, b, n + 1))
                    if g == 0 and s > 0:
                        act.wait_ge(up_ok, nth(up_ok, b, s))
                    act.activation(a_hl[:, g * GRP:(g + 1) * GRP, 0, :], attn[g % 2],
                                   ACT.Identity).then_inc(ahi_ok, 1)

                take_block(b, 17)
                take_block(b, 19)
                exponentials(0, 0)
                take_block(b, 21)
                take_block(b, 22)
                high(0, 0)
                take_block(b, 24)
                take_block(b, 26)
                exponentials(0, 1)
                take_block(b, 28)
                high(0, 1)
                take_block(b, 30)
                exponentials(0, 2)
                for s in range(STAGES):
                    for g in range(3 if s == 0 else 0, NG + 1):
                        if g < NG:
                            exponentials(s, g)
                        if g >= 1:
                            high(s, g - 1)
                    act.wait_ge(up_ok, nth(up_ok, b, s + 1))
                    act.activation(upd, up_ps, ACT.Identity).then_inc(upc_ok, 1)
                    act.wait_ge(fold_ok, nth(fold_ok, b, s + 1))
                    act.wait_ge(upc_ok, nth(upc_ok, b, s + 1))
                    act.activation(upd, up_ps, ACT.Square, accum_out=n2).then_inc(n2_ok, 1)
                    if s < STAGES - 1:
                        act.wait_ge(bt_ok, nth(bt_ok, b, s + 1))
                        act.activation(b_hl[:, :, 0, :], up_t, ACT.Identity).then_inc(bhi_ok, 1)
                    else:
                        for g in range(2, NG):
                            act.wait_ge(tra_ok, nth(tra_ok, b, g + 1))
                            act.activation(aT[:, g * GRP:(g + 1) * GRP, :],
                                           tr_ps[g % 2].rearrange("p (i n) -> p i n", n=P),
                                           ACT.Identity).then_inc(aTa_ok, 1)
                        act.wait_ge(base_ok, nth(base_ok, b, s + 1))
                        act.activation(bT[:, 0, :], base, ACT.Identity).then_inc(bhi_ok, 1)
                squares(b, 0)
                act.wait_ge(blo_ok, nth(blo_ok, b, STAGES))
                diagonals(b, 0)
                for j in range(NR):
                    image(b, 0, j)
                squares(b, 1)
                for t in range(T):
                    for j in range(NR):
                        hidden(b, t, j)
                        if j == 0 and t + 1 < T:
                            diagonals(b, t + 1)
                        if j == 2 and t + 2 < T:
                            squares(b, t + 2)
                for u in range(T):
                    for j in range(NC):
                        if not last and u == T - 1:
                            for e in (2 * j - 4, 2 * j - 3):
                                if e >= 0 and EV_OWNER[e] == 'a':
                                    take_block(b + 1, e)
                        result(b, u, j)
                        if j > 0:
                            over(b, u, j - 1)
                        if j == NC - 1:
                            over(b, u, j)
                        for k, at in enumerate(((1, 4), (1, 5), (2, 4), (2, 5), (3, 4), (3, 5))):
                            if not last and (u, j) == at:
                                hi_a(b + 1, k // 2, k % 2, b)
                if not last:
                    for e in range(EARLY - 4, EARLY):
                        if EV_OWNER[e] == 'a':
                            take_block(b + 1, e)
                    for h in range(2):
                        hi_a(b + 1, T - 1, h, b)

            for t in range(T):
                act.wait_ge(setup_t, 3 + t)
                act.activation(w16[:, t, 0, :], banks[:, t, :], ACT.Identity).then_inc(setup_a, 1)
            for t in range(T):
                hi_a(0, t, 0, None)
                hi_a(0, t, 1, None)
            for e in range(EARLY):
                if EV_OWNER[e] == 'a':
                    take_block(0, e)
            with act.Fori(0, B - 1) as b:
                body(b, False)
            body(B - 1, True)

        @block.vector
        def _(dve):
            def stats_a(batch, t):
                dve.wait_ge(x_in[t], nth(x_in[t], batch, 1))
                for j in range(NC):
                    ins = dve.bn_stats(bn_s[:, j, :], x_st[t][:, j * MM:(j + 1) * MM])
                ins.then_inc(bns_ok, 1)
                dve.wait_ge(bns_ok, nth(bns_ok, batch, t + 1))
                dve.sem_inc(gate, 1)
                dve.bn_aggr(mv, bn_s[:].rearrange("p j s -> p (j s)")).then_inc(a_stat, 1)

            def spread_a(batch, t):
                dve.wait_ge(a_gm, nth(a_gm, batch, t + 1))
                dve.tensor_copy(gm, st_ps).then_inc(gmc_ok, 1)
                dve.wait_ge(gmc_ok, nth(gmc_ok, batch, t + 1))
                dve.tensor_tensor(dev, mv[:, 0:1], gm[:, 0:1], ALU.subtract).then_inc(dif_ok, 1)
                dve.wait_ge(dif_ok, nth(dif_ok, batch, t + 1))
                dve.tensor_tensor(dev, dev, dev, ALU.mult).then_inc(a_dev, 1)

            def scale_a(batch, t):
                dve.wait_ge(a_gv, nth(a_gv, batch, t + 1))
                dve.tensor_scalar(var_a, sd_ps, gm[:, 1:2], EPS_GN, ALU.add, ALU.add).then_inc(a_var, 1)
                dve.wait_ge(a_pow, nth(a_pow, batch, t + 1))
                dve.scalar_tensor_tensor(nb_a, gm[:, 0:1], -1.0, s_a, ALU.mult, ALU.mult).then_inc(a_nb, 1)
                dve.wait_ge(a_nb, nth(a_nb, batch, t + 1))
                dve.tensor_scalar(x_st[t], x_st[t], s_a, nb_a, ALU.mult, ALU.add).then_inc(a_norm, 1)

            def low_a(batch, t):
                dve.wait_ge(a_hi, nth(a_hi, batch, 2 * t + 2))
                dve.tensor_tensor(halves[t][:, 1, LOP:N], x_st[t][:, LOP:N],
                                  halves[t][:, 0, LOP:N], ALU.subtract).then_inc(a_lov, 1)

            def take_block(b, e):
                dve.wait_ge(trx_ok, nth(trx_ok, b, e + 1))
                dve.tensor_copy(place_T(e),
                                tr_ps[e % 3].rearrange("p (i s c) -> p i s c", s=2, c=P)).then_inc(evv_ok, 1)

            def softmax(b, n, g):
                dve.wait_ge(lg_ok, nth(lg_ok, b, n + 1))
                if n > 0:
                    dve.wait_ge(sub_ok, nth(sub_ok, b, n))
                dve.tensor_reduce(mx, lg_ps[g], AX.X, ALU.max).then_inc(max_ok, 1)
                dve.wait_ge(max_ok, nth(max_ok, b, n + 1))
                dve.tensor_tensor(logit[g % 2], lg_ps[g],
                                  mx.unsqueeze(2).to_broadcast([P, GRP, K]), ALU.subtract).then_inc(sub_ok, 1)

            def normalise(b, n, g):
                dve.wait_ge(exp_ok, nth(exp_ok, b, n + 1))
                if n > 0:
                    dve.wait_ge(att_ok, nth(att_ok, b, n))
                dve.tensor_reduce(sm, logit[g % 2], AX.X, ALU.add).then_inc(sm_ok, 1)
                dve.wait_ge(sm_ok, nth(sm_ok, b, n + 1))
                dve.reciprocal(ri, sm).then_inc(ri_ok, 1)
                dve.wait_ge(ri_ok, nth(ri_ok, b, n + 1))
                if n >= 2:
                    dve.wait_ge(alo_ok, nth(alo_ok, b, n - 1))
                    dve.wait_ge(asum_ok, nth(asum_ok, b, n - 1))
                dve.scalar_tensor_tensor(attn[g % 2], logit[g % 2], ATTN_SCALE,
                                         ri.unsqueeze(2).to_broadcast([P, GRP, K]),
                                         ALU.mult, ALU.mult).then_inc(att_ok, 1)

            def total(b, n, g):
                dve.wait_ge(att_ok, nth(att_ok, b, n + 1))
                dve.tensor_reduce(asum[:, g, :], attn[g % 2].rearrange("p i k -> p k i"), AX.X,
                                  ALU.add).then_inc(asum_ok, 1)

            def rebase(b, s):
                dve.wait_ge(ssum_ok, nth(ssum_ok, b, s + 1))
                dve.tensor_scalar(den, sum_ps, EPS_NORM * ATTN_SCALE, EPS_NORM, ALU.add, ALU.mult).then_inc(den_ok, 1)
                dve.wait_ge(den_ok, nth(den_ok, b, 3 * s + 1))
                dve.wait_ge(rt_ok, nth(rt_ok, b, s + 1))
                dve.tensor_tensor(den, den, rt, ALU.add).then_inc(den_ok, 1)
                dve.wait_ge(den_ok, nth(den_ok, b, 3 * s + 2))
                dve.reciprocal(den, den).then_inc(den_ok, 1)
                dve.wait_ge(den_ok, nth(den_ok, b, 3 * s + 3))
                dve.tensor_scalar(base, up_ps, den, BASE_SCALE, ALU.mult, ALU.mult).then_inc(base_ok, 1)
                if s < STAGES - 1:
                    dve.wait_ge(bhi_ok, nth(bhi_ok, b, s + 1))
                    dve.tensor_tensor(b_hl[:, :, 1, :], up_t, b_hl[:, :, 0, :], ALU.subtract).then_inc(blo_ok, 1)
                else:
                    dve.wait_ge(bhi_ok, nth(bhi_ok, b, s + 1))
                    dve.tensor_tensor(bT[:, 1, :], base, bT[:, 0, :], ALU.subtract).then_inc(blo_ok, 1)

            def add_x(b, t, j):
                if j % 2 == 0:
                    dve.wait_ge(xr_in[j // 2], nth(xr_in[j // 2], b, t + 1))
                dve.wait_ge(rec_ok, nth(rec_ok, b, t * NC + j + 1))
                dve.scalar_tensor_tensor(
                    feat[:, t, j * MM:(j + 1) * MM], mm_ps[(t * NC + j) % 6] if t < 2 else rc_ps,
                    1.0 / (BASE_SCALE * ATTN_SCALE), stage[:, j * MM:(j + 1) * MM], ALU.mult, ALU.add,
                    accum_out=sums[t][:, j:j + 1]).then_inc(x1_ok, 1)

            def sum_c(b, t):
                dve.wait_ge(x1_ok, nth(x1_ok, b, (t + 1) * NC))
                dve.tensor_reduce(sm1[t], sums[t], AX.X, ALU.add).then_inc(c_sum, 1)

            def mean_c(b, t):
                dve.wait_ge(c_gm, nth(c_gm, b, t + 1))
                dve.tensor_scalar(nmg[t], st_ps[:, 0:1], -INV_N, None, ALU.mult).then_inc(c_nmg, 1)

            def var_c_(b, t):
                dve.wait_ge(c_gv, nth(c_gv, b, t + 1))
                dve.tensor_scalar(var_c[t], sd_ps, INV_N, EPS_GN, ALU.mult, ALU.add).then_inc(c_var, 1)

            def bias_c(b, t):
                dve.wait_ge(c_pow, nth(c_pow, b, t + 1))
                dve.tensor_tensor(nb_c[t], nmg[t], s_c[t], ALU.mult).then_inc(c_nb, 1)

            def depthwise(b, n):
                t, j = n // NR, n % NR
                dve.wait_ge(dwp_ok, nth(dwp_ok, b, n + 1))
                for i, k in enumerate(range(PE_TAPS, 9)):
                    dy, dx = k // 3, k % 3
                    if i > 0:
                        dve.wait_ge(tap_ok, nth(tap_ok, b, n * DVE_TAPS + i))
                    dve.scalar_tensor_tensor(
                        dw_ps[n % 3], img[:, j * ROWS + dy:(j + 1) * ROWS + dy, dx:dx + WW],
                        taps[:, t, k:k + 1], dw_ps[n % 3], ALU.mult, ALU.add).then_inc(tap_ok, 1)
                    c = 2 * NC + NC // 2 + 2 * n + i // 2
                    if i in (1, 3) and c - i // 2 + 1 < T * NC:
                        add_x(b, c // NC, c % NC)
                    if i == 2 and n % NR == 2 and n < NC:
                        mean_c(b, 2 + n // NR)
                    if i == 2 and n % NR == 0 and n < 3 * NR:
                        var_c_(b, 1 + n // NR)
                if n % NR == 1 and n < NC:
                    sum_c(b, 2 + n // NR)
                if n % NR == 0 and n < 3 * NR:
                    bias_c(b, 1 + n // NR)

            def prune(b, t):
                dve.wait_ge(hov_ok, nth(hov_ok, b, (t + 1) * NR))
                dve.tensor_reduce(hm1, hov[t % 2], AX.X, ALU.add).then_inc(hmax_ok, 1)
                dve.wait_ge(hmax_ok, nth(hmax_ok, b, t + 1))
                dve.tensor_scalar(mask1[:, t:t + 1], hm1, 0.0, None, ALU.is_gt).then_inc(mask1_ok, 1)
                dve.wait_ge(mask1_ok, nth(mask1_ok, b, t + 1))
                if t == 0:
                    dve.wait_ge(wl_in, nth(wl_in, b, 1))
                dve.tensor_scalar(w16[:, t], w16[:, t], mask1[:, t:t + 1], None, ALU.mult).then_inc(w_ok, 1)

            def finish(b, u):
                dve.wait_ge(rov_ok, nth(rov_ok, b, (u + 1) * NC))
                dve.tensor_reduce(rm1, rov[u % 2], AX.X, ALU.add).then_inc(rmax_ok, 1)
                dve.wait_ge(rmax_ok, nth(rmax_ok, b, u + 1))
                dve.tensor_scalar(mask2, rm1, 0.0, None, ALU.is_gt).then_inc(mask2_ok, 1)
                dve.wait_ge(mask2_ok, nth(mask2_ok, b, u + 1))
                for h in range(2):
                    px = slice(h * N // 2, (h + 1) * N // 2)
                    dve.scalar_tensor_tensor(feat[:, u, px], res[:, px], mask2, feat[:, u, px],
                                             ALU.mult, ALU.add).then_inc(y_ok, 1)

            def body(b, last):
                softmax(b, 0, 0)
                normalise(b, 0, 0)
                take_block(b, 23)
                total(b, 0, 0)
                take_block(b, 25)
                softmax(b, 1, 1)
                take_block(b, 27)
                normalise(b, 1, 1)
                take_block(b, 29)
                take_block(b, 31)
                total(b, 1, 1)
                softmax(b, 2, 2)
                for s in range(STAGES):
                    for g in range(3 if s == 0 else 0, NG + 1):
                        if g < NG:
                            softmax(b, s * NG + g, g)
                        if g >= 1:
                            normalise(b, s * NG + g - 1, g - 1)
                            total(b, s * NG + g - 1, g - 1)
                    if s == STAGES - 1:
                        for g in range(2):
                            dve.wait_ge(tra_ok, nth(tra_ok, b, g + 1))
                            dve.tensor_copy(aT[:, g * GRP:(g + 1) * GRP, :],
                                            tr_ps[g % 2].rearrange("p (i n) -> p i n", n=P)).then_inc(aTv_ok, 1)
                    rebase(b, s)
                for j in range(NC):
                    add_x(b, 0, j)
                sum_c(b, 0)
                mean_c(b, 0)
                for j in range(NC):
                    if j == 6:
                        var_c_(b, 0)
                    add_x(b, 1, j)
                    if j == 6:
                        bias_c(b, 0)
                sum_c(b, 1)
                mean_c(b, 1)
                for j in range(NC // 2):
                    add_x(b, 2, j)
                for n in range(T * NR):
                    depthwise(b, n)
                    if n % NR == 2 and n > NR:
                        prune(b, n // NR - 1)
                prune(b, T - 1)
                if last:
                    for u in range(T):
                        finish(b, u)
                else:
                    nb = b + 1
                    stats_a(nb, 0)
                    spread_a(nb, 0)
                    scale_a(nb, 0)
                    stats_a(nb, 1)
                    finish(b, 0)
                    spread_a(nb, 1)
                    scale_a(nb, 1)
                    low_a(nb, 0)
                    finish(b, 1)
                    stats_a(nb, 2)
                    spread_a(nb, 2)
                    low_a(nb, 1)
                    scale_a(nb, 2)
                    finish(b, 2)
                    take_block(nb, 0)
                    take_block(nb, 1)
                    take_block(nb, 3)
                    stats_a(nb, 3)
                    take_block(nb, 5)
                    spread_a(nb, 3)
                    scale_a(nb, 3)
                    take_block(nb, 8)
                    take_block(nb, 9)
                    low_a(nb, 2)
                    take_block(nb, 12)
                    take_block(nb, 13)
                    take_block(nb, 15)
                    finish(b, 3)
                    low_a(nb, 3)
                    for e in (16, 18, 20):
                        take_block(nb, e)

            n = [0]

            def step(ins):
                n[0] += 1
                ins.then_inc(setup_v, 1)
                dve.wait_ge(setup_v, n[0])

            dve.wait_ge(setup_t, 1)
            step(dve.tensor_copy(prm[:], banks[:, 7, 0:10 * T].rearrange("p (i t) -> p i t", t=T)))
            step(dve.tensor_scalar(prm[:, V1, :], prm[:, V1, :], EPS_BN, None, ALU.add))
            step(dve.tensor_scalar(prm[:, V2, :], prm[:, V2, :], EPS_BN, None, ALU.add))
            dve.wait_ge(setup_p, 3)
            step(dve.tensor_tensor(prm[:, G1, :], prm[:, G1, :], prm[:, V1, :], ALU.mult))
            step(dve.tensor_tensor(prm[:, G2, :], prm[:, G2, :], prm[:, V2, :], ALU.mult))
            step(dve.tensor_tensor(prm[:, DWB:DWB + 1, :], prm[:, DWB:DWB + 1, :], prm[:, M1:M1 + 1, :], ALU.subtract))
            step(dve.tensor_tensor(prm[:, PWB, :], prm[:, PWB, :], prm[:, M2, :], ALU.subtract))
            step(dve.tensor_tensor(prm[:, DWB, :], prm[:, DWB, :], prm[:, G1, :], ALU.mult))
            step(dve.tensor_tensor(prm[:, PWB, :], prm[:, PWB, :], prm[:, G2, :], ALU.mult))
            dve.wait_ge(bas_in, 16)
            step(dve.tensor_tensor(work[:, 2, 0:T * K], work[:, 0, 0:T * K], work[:, 0, 0:T * K], ALU.mult))
            dve.wait_ge(setup_t, 2)
            step(dve.tensor_copy(work[:, 1, 0:K], up_ps[:, 0:K]))
            dve.wait_ge(setup_p, 4)
            step(dve.tensor_scalar(work[:, 1, 0:K], work[:, 1, 0:K], EPS_NORM, None, ALU.add))
            step(dve.reciprocal(work[:, 1, 0:K], work[:, 1, 0:K]))
            for t in range(T):
                step(dve.scalar_tensor_tensor(work[:, 0, t * K:(t + 1) * K], work[:, 0, t * K:(t + 1) * K],
                                              BASE_SCALE, work[:, 1, 0:K], ALU.mult, ALU.mult))
                step(dve.tensor_copy(b0_hl[:, t, 0, :], work[:, 0, t * K:(t + 1) * K]))
                dve.tensor_tensor(b0_hl[:, t, 1, :], work[:, 0, t * K:(t + 1) * K], b0_hl[:, t, 0, :], ALU.subtract)
                dve.wait_ge(setup_a, t + 1)
                step(dve.tensor_tensor(w16[:, t, 1, :], banks[:, t, :], w16[:, t, 0, :], ALU.subtract))
                step(dve.tensor_scalar(taps[:, t, :], taps[:, t, :], prm[:, G1, t:t + 1], None, ALU.mult))
            assert n[0] == SETUP_V, n[0]
            dve.tensor_tensor(c1[:], prm[:, DWB, :], prm[:, B1, :], ALU.add)
            dve.tensor_tensor(c2[:], prm[:, PWB, :], prm[:, B2, :], ALU.add)
            dve.tensor_scalar(i2[:], prm[:, G2, :], 1.0 / PW_SCALE, None, ALU.mult).then_inc(setup_v, 1)
            for t in range(T):
                stats_a(0, t)
                spread_a(0, t)
                scale_a(0, t)
                low_a(0, t)
            for e in range(EARLY + 5):
                if EV_OWNER[e] == 'v':
                    take_block(0, e)
            with dve.Fori(0, B - 1) as b:
                body(b, False)
            body(B - 1, True)

        @block.tensor
        def _(pe):
            mm = nc.tensor.matmul

            def stat_a(batch, t):
                pe.wait_ge(a_stat, nth(a_stat, batch, t + 1))
                mm(st_ps, gavg[:], mv, start=True, stop=True).then_inc(a_gm, 1)

            def spread_a(batch, t):
                pe.wait_ge(a_dev, nth(a_dev, batch, t + 1))
                mm(sd_ps, gavg[:], dev, start=True, stop=True).then_inc(a_gv, 1)

            def logits(bh, g, tiles):
                for i in range(GRP):
                    nt = g * GRP + i
                    px = slice(nt * P, (nt + 1) * P)
                    for t in tiles:
                        for fs, bs in ((0, 0), (0, 1), (1, 0)):
                            ins = mm(lg_ps[g][:, i, :], halves[t][:, fs, px], bh[:, t, bs, :],
                                     start=(i == 0 and t == 0 and fs + bs == 0),
                                     stop=(t == T - 1 and fs == 1), skip_group_check=True)
                return ins

            def turn_block(b, e):
                if e >= 3:
                    own, ev = (evv_ok, EV_NTH[e - 3]) if EV_OWNER[e - 3] == 'v' else (eva_ok, EV_NTH[e - 3])
                    pe.wait_ge(own, nth(own, b, ev))
                pe.sem_inc(gate, 1)
                t, blk = BLOCKS[e]
                out_v = tr_ps[e % 3].rearrange("p (i s c) -> p i s c", s=2, c=P)
                for i in range(4):
                    for fs in range(2):
                        px = slice((4 * blk + i) * P, (4 * blk + i + 1) * P)
                        ins = nc.tensor.transpose(out_v[:, i, fs, :], halves[t][:, fs, px], ident16[:])
                ins.then_inc(trx_ok, 1)

            def turn_attn(b, g):
                pe.wait_ge(alo_ok, nth(alo_ok, b, (STAGES - 1) * NG + g + 1))
                if g >= 2:
                    pe.wait_ge(aTv_ok, nth(aTv_ok, b, g - 1))
                pe.sem_inc(gate, 1)
                for i in range(GRP):
                    ins = nc.tensor.transpose(tr_ps[g % 2][:, i * P:(i + 1) * P],
                                              a_hl[:, g * GRP + i].rearrange("p s k -> p (s k)"), ident16[:])
                ins.then_inc(tra_ok, 1)

            def update(b, s, g):
                for i in range(GRP):
                    nt = g * GRP + i
                    first, end = nt == 0, nt == NT - 1
                    mm(up_ps, a_hl[:, nt].rearrange("p s k -> p (s k)"), featT[:, nt, 0, :],
                       start=first, stop=False, skip_group_check=True)
                    ins = mm(up_ps[0:K], a_hl[:, nt, 0, :], featT[:, nt, 1, :],
                             start=False, stop=end, skip_group_check=True)
                return ins

            def recon(b, c):
                t, j = c // NC, c % NC
                o = mm_ps[c % 6] if t < 2 else rc_ps
                if t >= 2:
                    pe.wait_ge(x1_ok, nth(x1_ok, b, c))
                elif c >= 6:
                    pe.wait_ge(x1_ok, nth(x1_ok, b, c - 5))
                mm(o, bT[:, 0, t * P:(t + 1) * P], aT[:, 4 * j:4 * j + 4, :], start=True, stop=False)
                mm(o, bT[0:K, 1, t * P:(t + 1) * P], aT[0:K, 4 * j:4 * j + 4, :],
                   start=False, stop=True).then_inc(rec_ok, 1)

            def depthwise(b, n):
                t, j = n // NR, n % NR
                if j == 0:
                    pe.wait_ge(diag_ok, nth(diag_ok, b, t + 1))
                if n < 2:
                    pe.wait_ge(x1_ok, nth(x1_ok, b, 2 * NC - 2 + 2 * n))
                if n >= 3:
                    pe.wait_ge(h32_ok, nth(h32_ok, b, n - 2))
                for h in range(2):
                    c = 2 * NC + NC // 2 + 2 * (n - 1) + h
                    if n > 0 and c < T * NC:
                        recon(b, c)
                    pe.wait_ge(img_ok, nth(img_ok, b, t * NR + min(j + 1 + h, NR)))
                    o = banks[:, 2 * (n % 3) + h, :].rearrange("p (h w) -> p h w", w=WW)
                    for k in range(PE_TAPS):
                        r = j * ROWS + h * ROWS // 2 + k // 3
                        ins = mm(o, diag[:, t % 2, k, :], img[:, r:r + ROWS // 2, k % 3:k % 3 + WW],
                                 start=(k == 0), stop=(k == PE_TAPS - 1))
                        if n == 0 and k % 2 == 0:
                            recon(b, 2 * NC + 2 * h + k // 2)
                ins.then_inc(dwp_ok, 1)

            def pointwise(b, u, j, tiles):
                n = u * NC + j
                for t in tiles:
                    if t == 0 and n >= 4:
                        pe.wait_ge(r_ok, nth(r_ok, b, n - 3))
                    elif t == 0:
                        pe.wait_ge(h32_ok, nth(h32_ok, b, T * NR - 2 + n // 2))
                    if t == T - 1 and u == 0:
                        pe.wait_ge(hlo_ok, nth(hlo_ok, b, t * NR + j // 2 + 1))
                    if n == 0:
                        pe.wait_ge(w_ok, nth(w_ok, b, t + 1))
                    for ws, hs in ((0, 0), (0, 1), (1, 0)):
                        ins = mm(pw_ps[n], w16[:, t, ws, u * P:(u + 1) * P], hid[:, j, t, hs, :],
                                 start=(t == 0 and ws + hs == 0), stop=(t == T - 1 and ws == 1))
                if tiles[-1] == T - 1:
                    ins.then_inc(pw_ok, 1)

            def body(b, last):
                for s in range(STAGES):
                    if s == 0:
                        for g in range(NG):
                            logits(b0_hl, g, [0])
                        for g in range(NG):
                            logits(b0_hl, g, [1])
                        pe.wait_ge(a_lov, nth(a_lov, b, T - 1))
                        pe.wait_ge(a_lop, nth(a_lop, b, T - 1))
                        for g in range(NG):
                            logits(b0_hl, g, [2])
                        for e in range(EARLY, EARLY + 5):
                            turn_block(b, e)
                        pe.wait_ge(a_lov, nth(a_lov, b, T))
                        pe.wait_ge(a_lop, nth(a_lop, b, T))
                        for g in range(NG):
                            logits(b0_hl, g, [T - 1]).then_inc(lg_ok, 1)
                        for e in range(EARLY + 5, NT):
                            turn_block(b, e)
                    else:
                        pe.wait_ge(blo_ok, nth(blo_ok, b, s))
                        for g in range(NG):
                            logits(b_hl, g, range(T)).then_inc(lg_ok, 1)
                    for g in range(NG):
                        pe.wait_ge(alo_ok, nth(alo_ok, b, s * NG + g + 1))
                        if s == 0:
                            done = max(NT - NC + 2 * g + 2, NT - 2)
                            pe.wait_ge(evv_ok, nth(evv_ok, b, EV_OWNER[:done].count('v')))
                            pe.wait_ge(eva_ok, nth(eva_ok, b, EV_OWNER[:done].count('a')))
                        ins = update(b, s, g)
                    ins.then_inc(up_ok, 1)
                    if s == STAGES - 1:
                        turn_attn(b, 0)
                        turn_attn(b, 1)
                    pe.wait_ge(asum_ok, nth(asum_ok, b, (s + 1) * NG))
                    for half in range(2):
                        for g in range(NG):
                            ins = mm(sum_ps[half * K:(half + 1) * K], asum[:, g, :], one_c,
                                     start=(g == 0), stop=(g == NG - 1))
                    ins.then_inc(ssum_ok, 1)
                    pe.wait_ge(upc_ok, nth(upc_ok, b, s + 1))
                    mm(up_ps, fold[:], upd, start=True, stop=True).then_inc(fold_ok, 1)
                    if s == STAGES - 1:
                        for g in range(2, NG):
                            turn_attn(b, g)
                    if s < STAGES - 1:
                        pe.wait_ge(base_ok, nth(base_ok, b, s + 1))
                        pe.wait_ge(n2_ok, nth(n2_ok, b, s + 1))
                        pe.sem_inc(gate, 1)
                        for t in range(T):
                            ins = nc.tensor.transpose(up_t[:, t, :], base[0:K, t * P:(t + 1) * P], ident[0:K, 0:K])
                        ins.then_inc(bt_ok, 1)
                pe.wait_ge(blo_ok, nth(blo_ok, b, STAGES))
                pe.wait_ge(aTv_ok, nth(aTv_ok, b, 2))
                pe.wait_ge(aTa_ok, nth(aTa_ok, b, 2))

                def mean_c(t):
                    pe.wait_ge(c_sum, nth(c_sum, b, t + 1))
                    if t > 0:
                        pe.wait_ge(c_var, nth(c_var, b, t))
                    mm(st_ps[:, 0:1], gavg[:], sm1[t], start=True, stop=True).then_inc(c_gm, 1)

                def var_c_(t):
                    pe.wait_ge(c_sq, nth(c_sq, b, t + 1))
                    mm(sd_ps, gavg[:], sq[t], start=True, stop=True).then_inc(c_gv, 1)

                for c in range(NC):
                    recon(b, c)
                mean_c(0)
                for c in range(NC, 2 * NC):
                    if c == 2 * NC - 1:
                        var_c_(0)
                    recon(b, c)
                mean_c(1)
                for n in range(T * NR):
                    if n % NR == 1 and n < 3 * NR:
                        var_c_(1 + n // NR)
                    if n % NR == 3 and n < NC:
                        mean_c(2 + n // NR)
                    depthwise(b, n)
                for j in range(4):
                    pointwise(b, 0, j, range(T - 1))
                for u in range(T):
                    for j in range(NC):
                        pointwise(b, u, j, [T - 1] if u * NC + j < 4 else range(T))
                        if last:
                            continue
                        for t, at in enumerate(((0, 3), (1, 0), (2, 6), (3, 4))):
                            if (u, j) == at:
                                stat_a(b + 1, t)
                        for t, at in enumerate(((0, 4), (1, 2), (2, 7), (3, 4))):
                            if (u, j) == at:
                                spread_a(b + 1, t)
                        if u == T - 1:
                            if j == 1:
                                pe.wait_ge(a_lov, nth(a_lov, b + 1, 2))
                                pe.wait_ge(a_lop, nth(a_lop, b + 1, 2))
                            for e in range(max(2 * j - 2, 0), 2 * j if j < NC - 1 else EARLY):
                                turn_block(b + 1, e)
                if not last:
                    pe.wait_ge(r_ok, nth(r_ok, b, T * NC))

            pe.wait_ge(const_ok, 1)
            pe.wait_ge(prm_in, 16 * 11)
            nc.tensor.transpose(banks[:, 7, 0:10 * T], prm_rows, ident[0:10 * T, 0:10 * T]).then_inc(setup_t, 1)
            pe.wait_ge(setup_v, 10)
            for t in range(T):
                ins = mm(up_ps[:, 0:K], onesf, work[:, 2, t * K:(t + 1) * K], start=(t == 0), stop=(t == T - 1))
            ins.then_inc(setup_t, 1)
            pe.wait_ge(w_in, 16)
            for t in range(T):
                for u in range(T):
                    ins = mm(banks[:, t, u * P:(u + 1) * P], stage[:, u * C + t * P:u * C + (t + 1) * P], scaled,
                             start=True, stop=True)
                ins.then_inc(setup_t, 1)
            for t in range(T):
                stat_a(0, t)
                spread_a(0, t)
            for e in range(EARLY):
                turn_block(0, e)
            with pe.Fori(0, B - 1) as b:
                body(b, False)
            body(B - 1, True)


_INS = ['x', 'L0_conv_bases', 'L1_conv_dw_w', 'L1_conv_dw_b', 'L1_conv_bn1_g', 'L1_conv_bn1_b', 'L1_conv_bn1_m',
        'L1_conv_bn1_v', 'L1_conv_pw_w', 'L1_conv_pw_b', 'L1_conv_bn2_g', 'L1_conv_bn2_b', 'L1_conv_bn2_m',
        'L1_conv_bn2_v']


def kernel(**inputs):
    import numpy as _np
    import concourse.bacc as _bacc
    from concourse import mybir as _mybir
    from concourse.bass_utils import run_bass_kernel_spmd as _run

    nc = _bacc.Bacc("TRN2", target_bir_lowering=False, num_devices=1)
    arrays, args = {}, []
    for name in _INS:
        a = _np.ascontiguousarray(inputs[name])
        arrays[f"in_{name}_dram"] = a
        args.append(nc.dram_tensor(f"in_{name}_dram", a.shape, _mybir.dt.from_np(a.dtype), kind="ExternalInput").ap())
    shape = inputs['x'].shape
    args.append(nc.dram_tensor("out_0_dram", shape, _mybir.dt.float32, kind="ExternalOutput").ap())
    conv_preact_block(nc, *args)
    r = _run(nc, [arrays], core_ids=[0])
    return r.results[0]["out_0_dram"]
```
